# Optimizing a Trainium2 kernel written in Bass

```python
import numpy as np
import jax
import jax.numpy as jnp

def _softmax(x, axis=-1):
    return jax.nn.softmax(x, axis=axis)

def _gelu(x):
    return jax.nn.gelu(x, approximate=True)

def _silu(x):
    return jax.nn.silu(x)

def _sigmoid(x):
    return jax.nn.sigmoid(x)

def _layernorm(x, axis=-1, eps=1e-05):
    m = jnp.mean(x, axis=axis, keepdims=True)
    v = jnp.var(x, axis=axis, keepdims=True)
    return (x - m) / jnp.sqrt(v + eps)

def _scatter_add(tgt, idx, src, axis=0):
    return tgt.at[idx].add(src)

def _segment_sum(src, seg, n):
    return jax.ops.segment_sum(src, seg, n)
kernel_name = 'mk_decoder_preln_d1_seqx_r4_dee2cc'

def setup_inputs(seed: int=0):
    np.random.seed(seed)
    _w = jnp.asarray

    def _rec_inputs():
        import jax
        import jax.numpy as jnp
        _rk = jax.random.key(seed)
        x = -0.0002928 + 1 * jax.random.normal(jax.random.fold_in(_rk, 1), (16, 512, 256), jnp.float32)
        _lenS = 512 - jax.random.randint(jax.random.fold_in(_rk, 7), (16,), 0, max(1, 512 // 4) + 1, jnp.int32)
        _lenS2 = 64 - jax.random.randint(jax.random.fold_in(_rk, 8), (16,), 0, max(1, 64 // 4) + 1, jnp.int32)
        _ctx_1024P = jax.random.normal(jax.random.fold_in(_rk, 11), (16, 16, 256), jnp.float32)
        _ctx_1024c = jax.random.dirichlet(jax.random.fold_in(_rk, 511), 0.3 * jnp.ones((16,), jnp.float32), (16, 64))
        _ctx_1024t = jnp.einsum('bsk,bkd->bsd', _ctx_1024c, _ctx_1024P)
        _ctx_1024t = _ctx_1024t * jax.lax.rsqrt(jnp.mean(jnp.square(_ctx_1024t)) + 1e-12) * 0.953939
        ctx_1024 = -1.78809e-06 + 0.0312453 * (_ctx_1024t + 0.3 * jax.random.normal(jax.random.fold_in(_rk, 611), (16, 64, 256), jnp.float32))
        return (x, ctx_1024)
    x, ctx_1024 = _rec_inputs()

    def _L0_attn_setup():
        import jax, jax.numpy as jnp
        import numpy as np
        key = jax.random.key(seed)
        ks = jax.random.split(key, 7)
        B, T, C = (8, 512, 256)
        s = 0.02
        return {'x': jax.random.normal(ks[0], (B, T, C), dtype=jnp.float32), 'Wq': jax.random.normal(ks[1], (C, C), dtype=jnp.float32) * s, 'bq': jax.random.normal(ks[2], (C,), dtype=jnp.float32) * s, 'Wk': jax.random.normal(ks[3], (C, C), dtype=jnp.float32) * s, 'bk': jax.random.normal(ks[4], (C,), dtype=jnp.float32) * s, 'Wv': jax.random.normal(ks[5], (C, C), dtype=jnp.float32) * s, 'bv': jax.random.normal(ks[6], (C,), dtype=jnp.float32) * s}
    _L0_attn_all = _L0_attn_setup()
    _L0_attn_in = {k: v for k, v in _L0_attn_all.items() if k in ('Wq', 'bq', 'Wk', 'bk', 'Wv', 'bv')}
    del _L0_attn_all

    def _L0_xattn_setup():
        import jax, jax.numpy as jnp
        import numpy as np
        E, TPE, H, F = (64, 64, 256, 256)
        key = jax.random.key(seed)
        k1, k2, k3, k4 = jax.random.split(key, 4)
        scale = 1.0 / np.sqrt(H)
        return {'x': jax.random.normal(k1, (E, TPE, H), dtype=jnp.float32), 'w1': jax.random.normal(k2, (E, F, H), dtype=jnp.float32) * scale, 'v1': jax.random.normal(k3, (E, F, H), dtype=jnp.float32) * scale, 'w2': jax.random.normal(k4, (E, F, H), dtype=jnp.float32) * scale}
    _L0_xattn_all = _L0_xattn_setup()
    _L0_xattn_in = {k: v for k, v in _L0_xattn_all.items() if k in ()}
    del _L0_xattn_all

    def _L0_ffn_setup():
        import jax, jax.numpy as jnp
        import numpy as np
        IN_FEATURES = 256
        ACT_BITS = 4

        def _hadamard(size: int) -> np.ndarray:
            h = np.array([[1.0]], dtype=np.float64)
            while h.shape[0] < size:
                h = np.block([[h, h], [h, -h]])
            return (h / np.sqrt(size)).astype(np.float32)

        def _quantize_activations(x, bits=ACT_BITS):
            pos = 2 ** (bits - 1) - 1
            neg = 2 ** (bits - 1)
            scale = jnp.clip(jnp.max(jnp.abs(jax.lax.stop_gradient(x)), axis=-1, keepdims=True), 1e-05) / pos
            q = jnp.clip(jnp.round(x / scale), -neg, pos) * scale
            return x + jax.lax.stop_gradient(q - x)

        def _ternary_quantize_ste(w):
            scale = jnp.clip(jnp.mean(jnp.abs(jax.lax.stop_gradient(w)), axis=1, keepdims=True), 1e-05)
            n = w / scale
            tern = jnp.where(n > 0.5, 1.0, jnp.where(n < -0.5, -1.0, 0.0))
            q = tern * scale
            return w + jax.lax.stop_gradient(q - w)
        key = jax.random.key(seed)
        k1, k2 = jax.random.split(key)
        x = jax.random.normal(k1, (8, 2048, IN_FEATURES), dtype=jnp.float32)
        bound = 1.0 / np.sqrt(IN_FEATURES)
        weight = jax.random.uniform(k2, (256, IN_FEATURES), dtype=jnp.float32, minval=-bound, maxval=bound)
        return {'x': x, 'weight': weight}
    _L0_ffn_all = _L0_ffn_setup()
    _L0_ffn_in = {k: v for k, v in _L0_ffn_all.items() if k in ('weight',)}
    del _L0_ffn_all
    return {'x': x, 'ctx_1024': ctx_1024, 'L0_attn_Wq': _L0_attn_in['Wq'], 'L0_attn_bq': _L0_attn_in['bq'], 'L0_attn_Wk': _L0_attn_in['Wk'], 'L0_attn_bk': _L0_attn_in['bk'], 'L0_attn_Wv': _L0_attn_in['Wv'], 'L0_attn_bv': _L0_attn_in['bv'], 'L0_ffn_weight': _L0_ffn_in['weight']}

def reference(x, ctx_1024, L0_attn_Wq, L0_attn_bq, L0_attn_Wk, L0_attn_bk, L0_attn_Wv, L0_attn_bv, L0_ffn_weight):
    import jax
    import jax.numpy as jnp

    def _L0_attn_ref(x, Wq, bq, Wk, bk, Wv, bv):
        import jax, jax.numpy as jnp
        import numpy as np
        B, T, C = x.shape
        q = x @ Wq.T + bq
        k = x @ Wk.T + bk
        v = x @ Wv.T + bv
        scale = jnp.asarray(C, x.dtype) ** (-0.5)
        att = jnp.einsum('btc,bsc->bts', q, k) * scale
        causal = jnp.tril(jnp.ones((T, T), dtype=bool))
        att = jnp.where(causal, att, jnp.finfo(att.dtype).min)
        att = jax.nn.softmax(att, axis=-1)
        out = jnp.einsum('bts,bsc->btc', att, v)
        return out

    def _L0_xattn_ref(x, w1, v1, w2):
        import jax, jax.numpy as jnp
        import numpy as np
        E, TPE, H, F = (64, 64, 256, 256)
        h1 = jnp.einsum('eth,efh->etf', x, w1)
        h2 = jnp.einsum('eth,efh->etf', x, v1)
        g = jax.nn.gelu(h1, approximate=False) * h2
        return jnp.einsum('etf,efh->eth', g, w2)

    def _L0_ffn_ref(x, weight):
        import jax, jax.numpy as jnp
        import numpy as np
        IN_FEATURES = 256
        ACT_BITS = 4

        def _hadamard(size: int) -> np.ndarray:
            h = np.array([[1.0]], dtype=np.float64)
            while h.shape[0] < size:
                h = np.block([[h, h], [h, -h]])
            return (h / np.sqrt(size)).astype(np.float32)

        def _quantize_activations(x, bits=ACT_BITS):
            pos = 2 ** (bits - 1) - 1
            neg = 2 ** (bits - 1)
            scale = jnp.clip(jnp.max(jnp.abs(jax.lax.stop_gradient(x)), axis=-1, keepdims=True), 1e-05) / pos
            q = jnp.clip(jnp.round(x / scale), -neg, pos) * scale
            return x + jax.lax.stop_gradient(q - x)

        def _ternary_quantize_ste(w):
            scale = jnp.clip(jnp.mean(jnp.abs(jax.lax.stop_gradient(w)), axis=1, keepdims=True), 1e-05)
            n = w / scale
            tern = jnp.where(n > 0.5, 1.0, jnp.where(n < -0.5, -1.0, 0.0))
            q = tern * scale
            return w + jax.lax.stop_gradient(q - w)
        H = jnp.asarray(_hadamard(IN_FEATURES))
        xh = x @ H
        xq = _quantize_activations(xh)
        wq = _ternary_quantize_ste(weight)
        return jnp.einsum('bsi,oi->bso', xq, wq)
    x = x + _L0_attn_ref(_layernorm(x, axis=-1), L0_attn_Wq, L0_attn_bq, L0_attn_Wk, L0_attn_bk, L0_attn_Wv, L0_attn_bv)
    x = x + _L0_xattn_ref(_layernorm(x, axis=-1), ctx_1024, ctx_1024, ctx_1024)
    x = x + _L0_ffn_ref(_layernorm(x, axis=-1), L0_ffn_weight)
    return x

_drawn_inputs = setup_inputs


def setup_inputs(seed=0):
    import zlib

    import numpy as np

    out = dict(_drawn_inputs(seed))
    spreads = {}
    factors = {'L0_attn_Wq': 4.689, 'L0_attn_bq': 8.0, 'L0_attn_Wk': 4.657, 'L0_attn_bk': 8.0}
    for name, (base, spread) in spreads.items():
        noise = np.random.default_rng([zlib.crc32(name.encode()), seed]).standard_normal(out[name].shape)
        drawn = base * np.exp(spread * noise) if base else spread * noise
        out[name] = jnp.asarray(drawn.astype(out[name].dtype))
    for name, factor in factors.items():
        out[name] = (out[name] * factor).astype(out[name].dtype)
    return out
```

```python
from contextlib import ExitStack

import numpy as np

import concourse.bass as bass
from concourse import mybir

F32 = mybir.dt.float32
F16 = mybir.dt.float16
BF16 = mybir.dt.bfloat16
I32 = mybir.dt.int32
ALU = mybir.AluOpType
ACT = mybir.ActivationFunctionType
AX = mybir.AxisListType

P = 128
LN_EPS = 1e-5
X_SCALE = 2.0 ** 8
W_SCALE = 2.0 ** 13
QV_SCALE = 2.0 ** -15
P_SCALE = 2.0 ** 14
G_MIN = 2.0 ** -35
ROUND = 1.5 * 2.0 ** 23
MASKED = -1e30
ACT_MAX = 7.0
QUANT_MIN = 1e-5


def upto(batch, per_batch, k):
    return batch * per_batch + k


def build(nc, x, ctx_kv, wq, bq, wk, wv, bv, wffn, hada, ident, ident16, mask, y):
    B, T, C = x.shape
    F = ctx_kv.shape[1]
    NT = T // P
    KC = C // P
    assert (NT, KC, F) == (4, 2, 64) and B % 2 == 0 and B >= 6
    SM_SCALE = float(C) ** -0.5
    Q_SCALE2 = QV_SCALE * W_SCALE * X_SCALE
    S_EXP = SM_SCALE / (Q_SCALE2 * X_SCALE)
    H_TRUE = 1.0 / (W_SCALE * X_SCALE)
    G_KEPT = 2.0 ** -3
    H_DIM = float(C) ** 0.5
    HAD_SCALE = X_SCALE * H_DIM

    es = ExitStack()
    with es:
        def sb(name, shape, dt):
            return es.enter_context(nc.sbuf_tensor(name, shape, dt))

        def sem(name):
            return es.enter_context(nc.semaphore(name))

        bank = [es.enter_context(nc.psum_tensor(f"bank{i}", [P, 512], F32)) for i in range(8)]

        wq_sb = sb("wq_sb", [P, KC, C], F32)
        wk_sb = sb("wk_sb", [P, KC, C], F32)
        wv_sb = sb("wv_sb", [P, KC, C], F32)
        bq_sb = sb("bq_sb", [P, KC], F32)
        bv_sb = sb("bv_sb", [64, C], F32)
        wf_sb = sb("wf_sb", [P, KC, C], F32)
        ctx_sb = sb("ctx_sb", [P, B, C], F32)
        had = sb("had", [P, KC, C], F16)
        idf = sb("idf", [P, P], F32)
        idh = sb("idh", [P, P], F16)
        msk = sb("msk", [P, P], BF16)
        m_hi = sb("m_hi", [P, KC, C], F16)
        m_lo = sb("m_lo", [P, KC, C], F16)
        wv_hi = sb("wv_hi", [P, KC, C], F16)
        wv_lo = sb("wv_lo", [P, KC, C], F16)
        bias_rows = sb("bias_rows", [P, 2, C], F16)
        one_rows = sb("one_rows", [P, T], F16)
        ctx_hi = sb("ctx_hi", [P, B, C], F16)
        ctx_lo = sb("ctx_lo", [P, B, C], F16)
        cT_hi = sb("cT_hi", [P, B, KC, P], F16)
        cT_lo = sb("cT_lo", [P, B, KC, P], F16)
        ternT = sb("ternT", [P, KC, C], F16)
        wsb = sb("wsb", [P, C], F32)
        ones = sb("ones", [P, P], F32)
        bqb = sb("bqb", [P, KC, 64], F32)
        red = sb("red", [P, 4], F32)
        redw = sb("redw", [P, 4], F32)
        gmax = sb("gmax", [P, 4], F32)
        pw = sb("pw", [P, 4], F32)
        pinv = sb("pinv", [P, 4], F32)
        wsc = sb("wsc", [P, 4], F32)
        row_tmp = sb("row_tmp", [64, 2, C], F16)
        wsum = sb("wsum", [P, KC], F32)
        wmean = sb("wmean", [P, KC], F32)
        thr = sb("thr", [P, 2, KC], F32)
        tern_p = sb("tern_p", [P, KC, C], F32)
        tern_n = sb("tern_n", [P, KC, C], F32)
        tern = sb("tern", [P, KC, C], F16)
        diag = sb("diag", [P, KC, P], F32)
        pw_sq = sb("pw_sq", [P, 1], F32)
        exp_scale = sb("exp_scale", [P, 1], F32)
        v_scale = sb("v_scale", [P, 1], F32)
        h_scale = sb("h_scale", [P, 1], F32)
        g_scale = sb("g_scale", [P, 1], F32)
        o2_scale = sb("o2_scale", [P, 1], F32)
        rnd = sb("rnd", [P, 1], F32)
        unrnd = sb("unrnd", [P, 1], F32)
        mhalf = sb("mhalf", [P, NT], F32)
        mone = sb("mone", [P, NT], F32)

        xb = [sb(f"x_{i}", [P, NT, C], F32) for i in range(2)]
        x2 = sb("x2", [P, NT, C], F32)
        x3 = [sb(f"x3_{i}", [P, NT, C], F32) for i in range(2)]
        ytmp = sb("ytmp", [P, NT, C], F32)
        xn = [sb(f"xn_{i}", [P, NT, C], F32) for i in range(3)]
        xT_hi = [sb(f"xT_hi_{i}", [P, KC, T], F16) for i in range(3)]
        xT_lo = [sb(f"xT_lo_{i}", [P, KC, T], F16) for i in range(3)]
        st = [sb(f"st_{i}", [P, NT, 6], F32) for i in range(3)]
        mv = [sb(f"mv_{i}", [P, NT, 2], F32) for i in range(3)]
        ve = [sb(f"ve_{i}", [P, NT], F32) for i in range(3)]
        nm = [sb(f"nm_{i}", [P, NT], F32) for i in range(3)]
        rs = [sb(f"rs_{i}", [P, NT], F32) for i in range(3)]
        q_hi = sb("q_hi", [P, KC, T], F16)
        q_lo = sb("q_lo", [P, KC, T], F16)
        v_hi = sb("v_hi", [P, NT, C], F16)
        v_lo = sb("v_lo", [P, NT, C], F16)
        negmax = sb("negmax", [P, NT], F32)
        ebias = sb("ebias", [P, NT], F32)
        prob = sb("prob", [P, NT, T], F32)
        psums = sb("psums", [P, NT], F32)
        prinv = sb("prinv", [P, NT], F32)
        oscale = sb("oscale", [P, NT], F32)
        pT_hi = sb("pT_hi", [P, NT, T], F16)
        pT_lo = sb("pT_lo", [P, NT, T], F16)
        gel = sb("gel", [P, T], F32)
        gbuf = sb("gbuf", [P, T], F32)
        ghl = sb("ghl", [P, T], F16)
        amax = sb("amax", [P, NT], F32)
        qs = sb("qs", [P, NT], F32)
        qinv = sb("qinv", [P, NT], F32)
        rounded = sb("rounded", [P, NT, C], F32)
        quant = sb("quant", [P, NT, C], F16)
        qT = sb("qT", [P, KC, T], F16)

        ld_w = sem("ld_w")
        ld_ctx = sem("ld_ctx")
        ld_x = sem("ld_x")
        st_y = sem("st_y")
        s_ones = sem("s_ones")
        s_bqb = sem("s_bqb")
        s_M = sem("s_M")
        s_w = sem("s_w")
        s_wvT = sem("s_wvT")
        s_red = sem("s_red")
        s_all = sem("s_all")
        s_sc = sem("s_sc")
        s_whi = sem("s_whi")
        s_wlo = sem("s_wlo")
        s_chi = sem("s_chi")
        s_clo = sem("s_clo")
        s_cT = sem("s_cT")
        s_cThi = sem("s_cThi")
        s_cTlo = sem("s_cTlo")
        s_tern = sem("s_tern")
        s_ternT = sem("s_ternT")
        s_ternc = sem("s_ternc")
        s_diag = sem("s_diag")
        s_wsb = sem("s_wsb")
        s_wsc = sem("s_wsc")
        s_dv = sem("s_dv")
        stats_ready = [sem(f"stats_ready_{i}") for i in range(3)]
        xn_ready = [sem(f"xn_ready_{i}") for i in range(3)]
        xT_psum = [sem(f"xT_psum_{i}") for i in range(3)]
        xT_hi_ready = [sem(f"xT_hi_ready_{i}") for i in range(3)]
        xT_ready = [sem(f"xT_ready_{i}") for i in range(3)]
        q_psum = sem("q_psum")
        q_hi_ready = sem("q_hi_ready")
        q_ready = sem("q_ready")
        v_psum = sem("v_psum")
        v_hi_ready = sem("v_hi_ready")
        v_ready = sem("v_ready")
        scores_psum = sem("scores_psum")
        max_ready = sem("max_ready")
        ebias_ready = sem("ebias_ready")
        prob_ready = sem("prob_ready")
        pT_psum = sem("pT_psum")
        pT_hi_ready = sem("pT_hi_ready")
        pT_ready = sem("pT_ready")
        rinv_ready = sem("rinv_ready")
        oscale_ready = sem("oscale_ready")
        att_psum = sem("att_psum")
        x2_ready = sem("x2_ready")
        h_psum = sem("h_psum")
        gelu_ready = sem("gelu_ready")
        g_ready = sem("g_ready")
        g_hi_ready = sem("g_hi_ready")
        g_lo_ready = sem("g_lo_ready")
        o2_psum = sem("o2_psum")
        x3_ready = sem("x3_ready")
        had_psum = sem("had_psum")
        amax_ready = sem("amax_ready")
        qs_ready = sem("qs_ready")
        qinv_ready = sem("qinv_ready")
        round_ready = sem("round_ready")
        quant_ready = sem("quant_ready")
        qT_psum = sem("qT_psum")
        qT_ready = sem("qT_ready")
        y_psum = sem("y_psum")
        ytmp_ready = sem("ytmp_ready")
        y_ready = sem("y_ready")

        x_v = x.rearrange("b (i p) c -> b p i c", p=P)
        y_v = y.rearrange("b (i p) c -> b p i c", p=P)
        N_W = 11

        def steps(eng, body):
            body(-1, 1, "Z")
            body(0, 0, "ZA")
            body(1, 1, "ZAB")
            with eng.Fori(1, B // 2 - 1) as pair:
                body(pair * 2, 0, "ZABC")
                body(pair * 2 + 1, 1, "ZABC")
            body(B - 2, 0, "ZABC")
            body(B - 1, 1, "ABC")
            body(B, 0, "BC")
            body(B + 1, 1, "C")

        block = es.enter_context(nc.Block())

        @block.sync
        def _(sp):
            def load_x(b, parity):
                sp.dma_start(xb[parity][:], x_v[b]).then_inc(ld_x, 16)

            load_x(0, 0)
            sp.dma_start(idf[:], ident).then_inc(ld_w, 16)
            sp.dma_start(wq_sb[:], wq.rearrange("(k p) c -> p k c", p=P)).then_inc(ld_w, 16)
            sp.dma_start(wk_sb[:], wk.rearrange("(k p) c -> p k c", p=P)).then_inc(ld_w, 16)
            sp.dma_start(bq_sb[:], bq).then_inc(ld_w, 16)
            sp.dma_start(wv_sb[:], wv.rearrange("(k p) c -> p k c", p=P)).then_inc(ld_w, 16)
            for r in (0, 32):
                sp.dma_start(bv_sb[r:r + 1, :], bv.rearrange("(a c) -> a c", a=1)).then_inc(ld_w, 16)
            sp.dma_start(wf_sb[:], wffn.rearrange("(k p) c -> p k c", p=P)).then_inc(ld_w, 16)
            sp.dma_start(had[:], hada.rearrange("(k p) c -> p k c", p=P)).then_inc(ld_w, 16)
            sp.dma_start(idh[:], ident16).then_inc(ld_w, 16)
            sp.dma_start(msk[:], mask).then_inc(ld_w, 16)

            def body(n, parity, stages):
                if "C" in stages:
                    sp.wait_ge(y_ready, upto(n - 2, 1, 1))
                    sp.dma_start(y_v[n - 2], x3[parity][:]).then_inc(st_y, 16)
                if stages == "Z":
                    sp.wait_ge(ld_x, 16)
                    load_x(1, 1)
                elif "A" in stages and "Z" in stages:
                    if isinstance(n, int) and n + 2 >= B:
                        return
                    sp.wait_ge(x2_ready, upto(n, NT, NT))
                    load_x(n + 2, parity)

            steps(sp, body)
            sp.wait_ge(st_y, 16 * B)

        @block.gpsimd
        def _(pool):
            nc.gpsimd.memset(ones[:], 1.0)
            nc.gpsimd.memset(rnd[:], ROUND)
            nc.gpsimd.memset(unrnd[:], -ROUND)
            nc.gpsimd.memset(mhalf[:], -0.5)
            nc.gpsimd.memset(mone[:], -1.0)
            nc.gpsimd.memset(bias_rows[:], 0.0)
            nc.gpsimd.memset(one_rows[:], 0.0).then_inc(s_ones, 1)
            for h in range(2):
                nc.gpsimd.dma_start(ctx_sb[h * F:(h + 1) * F], ctx_kv.rearrange("b f c -> f b c"))\
                    .then_inc(ld_ctx, 16)
            pool.wait_ge(s_ones, 1)
            nc.gpsimd.memset(one_rows[0:1, :], X_SCALE)
            nc.gpsimd.memset(one_rows[32:33, :], X_SCALE).then_inc(s_ones, 1)
            pool.wait_ge(s_ones, 2)
            pool.wait_ge(s_red, 1)
            nc.gpsimd.partition_all_reduce(gmax[:, 0:3], red[:, 0:3], P, bass.bass_isa.ReduceOp.max)\
                .then_inc(s_all, 1)

            def normalise(k, b, src):
                pool.wait_ge(stats_ready[k], upto(b, 1, 1))
                nc.gpsimd.tensor_tensor(nm[k][:], mv[k][:, :, 0], mone[:], ALU.mult)
                nc.gpsimd.tensor_scalar(ve[k][:], mv[k][:, :, 1], X_SCALE ** -2, LN_EPS * X_SCALE ** -2,
                                        ALU.mult, ALU.add)
                pool.drain()
                nc.gpsimd.tensor_tensor(rs[k][:], ve[k][:], mhalf[:], ALU.pow)
                pool.drain()
                for i in range(NT):
                    nc.gpsimd.tensor_scalar(xn[k][:, i, :], src[:, i, :], nm[k][:, i:i + 1],
                                            rs[k][:, i:i + 1], ALU.add, ALU.mult).then_inc(xn_ready[k], 1)

            def body(n, parity, stages):
                if "B" in stages:
                    normalise(1, n - 1, x2)
                if "Z" in stages:
                    normalise(0, n + 1, xb[1 - parity])
                if "B" in stages:
                    normalise(2, n - 1, x3[1 - parity])
                if "C" in stages:
                    pool.wait_ge(ytmp_ready, upto(n - 2, NT, NT))
                    nc.gpsimd.tensor_tensor(x3[parity][:], x3[parity][:], ytmp[:], ALU.add)\
                        .then_inc(y_ready, 1)

            steps(pool, body)

        @block.scalar
        def _(act):
            act.wait_ge(s_sc, 1)
            nc.scalar.activation(m_hi[:], bank[0][:].rearrange("p (k c) -> p k c", k=KC), ACT.Copy,
                                 scale=wsc[:, 0:1]).then_inc(s_whi, 1)
            act.wait_ge(s_wvT, 1)
            nc.scalar.activation(wv_hi[:], bank[2][:].rearrange("p (k c) -> p k c", k=KC), ACT.Copy,
                                 scale=wsc[:, 1:2]).then_inc(s_whi, 1)
            for r in range(B // 2):
                act.wait_ge(s_cT, r + 1)
                nc.scalar.activation(cT_hi[:, 2 * r:2 * r + 2],
                                     bank[4 + r % 4][:].rearrange("p (b k f) -> p b k f", b=2, k=KC),
                                     ACT.Copy, scale=wsc[:, 2:3]).then_inc(s_cThi, 1)
            nc.scalar.activation(ctx_hi[:], ctx_sb[:], ACT.Copy, scale=wsc[:, 2:3]).then_inc(s_chi, 1)
            act.wait_ge(s_ternT, 1)
            nc.scalar.activation(ternT[:], bank[3].bitcast(F16)[:, 0:512].rearrange("p (k c) -> p k c", k=KC),
                                 ACT.Copy).then_inc(s_ternc, 1)
            act.wait_ge(s_wsb, 1)
            nc.scalar.activation(wsb[:], bank[1][:, 256:512], ACT.Copy, scale=1.0 / HAD_SCALE)\
                .then_inc(s_ternc, 1)
            act.wait_ge(s_ones, 2)

            def hi_transposed(k, b, banks):
                for kc in range(KC):
                    act.wait_ge(xT_psum[k], upto(b, KC, kc + 1))
                    nc.scalar.activation(xT_hi[k][:, kc, :], bank[banks[kc]][:], ACT.Copy)\
                        .then_inc(xT_hi_ready[k], 1)

            def exps(b, tiles):
                for i in tiles:
                    w = (i + 1) * P
                    act.wait_ge(ebias_ready, upto(b, 2, i // 2 + 1))
                    nc.scalar.activation(prob[:, i, 0:w], bank[4 + i % 2][:, 0:w], ACT.Exp,
                                         bias=ebias[:, i:i + 1], scale=exp_scale[:, 0:1],
                                         accum_out=psums[:, i:i + 1]).then_inc(prob_ready, 1)

            def prob_hi(b, tiles):
                for i in tiles:
                    w = (i + 1) * P
                    act.wait_ge(pT_psum, upto(b, NT, i + 1))
                    nc.scalar.activation(pT_hi[:, i, 0:w], bank[1 - i % 2][:, 0:w], ACT.Copy,
                                         scale=P_SCALE).then_inc(pT_hi_ready, 1)

            def body(n, parity, stages):
                if "A" in stages:
                    for kc in range(KC):
                        act.wait_ge(q_psum, upto(n, KC, kc + 1))
                        nc.scalar.activation(q_hi[:, kc, :], bank[2 + kc][:], ACT.Copy,
                                             scale=QV_SCALE).then_inc(q_hi_ready, 1)
                    for j in range(2):
                        act.wait_ge(v_psum, upto(n, 2, j + 1))
                        nc.scalar.activation(v_hi[:, 2 * j:2 * j + 2, :],
                                             bank[4 + j][:].rearrange("p (i c) -> p i c", i=2), ACT.Copy,
                                             scale=QV_SCALE).then_inc(v_hi_ready, 1)
                if "B" in stages:
                    hi_transposed(1, n - 1, (0, 1))
                if "C" in stages:
                    hi_transposed(2, n - 2, (6, 7))
                if "A" in stages:
                    exps(n, (0, 1))
                if "B" in stages:
                    act.wait_ge(h_psum, upto(n - 1, 1, 1))
                    nc.scalar.activation(gel[:], bank[0][:], ACT.Gelu, scale=h_scale[:, 0:1])\
                        .then_inc(gelu_ready, 1)
                    act.wait_ge(g_ready, upto(n - 1, 1, 1))
                    nc.scalar.activation(ghl[:], gbuf[:], ACT.Copy).then_inc(g_hi_ready, 1)
                if "C" in stages:
                    act.wait_ge(qinv_ready, upto(n - 2, 1, 1))
                    for i in range(NT):
                        nc.scalar.activation(rounded[:, i, :], bank[2 + i // 2][:, (i % 2) * C:(i % 2 + 1) * C],
                                             ACT.Identity, bias=rnd[:, 0:1], scale=qinv[:, i:i + 1])\
                            .then_inc(round_ready, 1)
                    act.wait_ge(round_ready, upto(n - 2, NT, NT))
                    nc.scalar.activation(quant[:], rounded[:], ACT.Identity, bias=unrnd[:, 0:1])\
                        .then_inc(quant_ready, 1)
                if "A" in stages:
                    exps(n, (2, 3))
                    prob_hi(n, (0, 1))
                if "C" in stages:
                    act.wait_ge(qT_psum, upto(n - 2, 1, 1))
                    nc.scalar.activation(qT[:], bank[2].bitcast(F16)[:, :].rearrange("p (k t) -> p k t", k=KC),
                                         ACT.Copy).then_inc(qT_ready, 1)
                if "A" in stages:
                    prob_hi(n, (2, 3))
                if "Z" in stages:
                    hi_transposed(0, n + 1, (4, 5))

            steps(act, body)

        @block.vector
        def _(dve):
            done = [0]

            def link(ins):
                done[0] += 1
                ins.then_inc(s_dv, 1)
                dve.wait_ge(s_dv, done[0])

            dve.wait_ge(ld_w, 16 * N_W)
            dve.wait_ge(s_ones, 2)
            for k in range(KC):
                ins = nc.vector.tensor_scalar(bqb[:, k, :], ones[:, 0:64], bq_sb[:, k:k + 1], None, ALU.mult)
            ins.then_inc(s_bqb, 1)

            def stats(k, b, src):
                for i in range(NT):
                    ins = nc.vector.bn_stats(st[k][:, i, :], src[:, i, :])
                dve.drain()
                for i in range(NT):
                    ins = nc.vector.bn_aggr(mv[k][:, i, :], st[k][:, i, :])
                ins.then_inc(stats_ready[k], 1)

            def setup():
                nc.vector.tensor_reduce(wsum[:], wf_sb[:], AX.X, ALU.add, apply_absolute_value=True)
                nc.vector.tensor_reduce(red[:, 1:2], wv_sb[:], AX.XY, ALU.max, apply_absolute_value=True)
                link(nc.vector.tensor_reduce(redw[0:1, 1:2], bv_sb[0:1, :], AX.X, ALU.max,
                                             apply_absolute_value=True))
                nc.vector.tensor_tensor(red[0:1, 1:2], red[0:1, 1:2], redw[0:1, 1:2], ALU.max)
                link(nc.vector.tensor_scalar(wmean[:], wsum[:], 1.0 / C, QUANT_MIN, ALU.mult, ALU.max))
                nc.vector.tensor_scalar(thr[:, 0, :], wmean[:], 0.5, None, ALU.mult)
                link(nc.vector.tensor_scalar(thr[:, 1, :], wmean[:], -0.5, None, ALU.mult))
                for k in range(KC):
                    nc.vector.tensor_scalar(diag[:, k, :], idf[:], wmean[:, k:k + 1], None, ALU.mult)
                    nc.vector.tensor_scalar(tern_p[:, k, :], wf_sb[:, k, :], thr[:, 0, k:k + 1], None, ALU.is_gt)
                    ins = nc.vector.tensor_scalar(tern_n[:, k, :], wf_sb[:, k, :], thr[:, 1, k:k + 1], None,
                                                  ALU.is_lt)
                link(ins)
                link(nc.vector.tensor_tensor(tern[:], tern_p[:], tern_n[:], ALU.subtract))
                nc.vector.engine_nop().then_inc(s_tern, 1)

                dve.wait_ge(s_w, 1)
                nc.vector.tensor_reduce(red[:, 0:1], bank[0][:], AX.X, ALU.max, apply_absolute_value=True)
                link(nc.vector.tensor_reduce(redw[0:64, 0:1], bank[1][0:64, 0:C], AX.X, ALU.max,
                                             apply_absolute_value=True))
                nc.vector.tensor_tensor(red[0:64, 0:1], red[0:64, 0:1], redw[0:64, 0:1], ALU.max)
                dve.wait_ge(ld_ctx, 32)
                nc.vector.tensor_reduce(red[:, 2:3], ctx_sb[:], AX.XY, ALU.max, apply_absolute_value=True)\
                    .then_inc(s_red, 1)

                dve.wait_ge(s_all, 1)
                link(nc.vector.tensor_scalar(gmax[:, 0:3], gmax[:, 0:3], G_MIN, None, ALU.max))
                link(nc.vector.tensor_scalar(pw[:, 0:3].bitcast(I32), gmax[:, 0:3].bitcast(I32), 0x7F800000, None,
                                             ALU.bitwise_and))
                nc.vector.tensor_scalar(exp_scale[:], pw[:, 0:1], S_EXP, None, ALU.mult)
                nc.vector.tensor_scalar(v_scale[:], pw[:, 1:2], 1.0 / (P_SCALE * Q_SCALE2), None, ALU.mult)
                nc.vector.tensor_scalar(h_scale[:], pw[:, 2:3], H_TRUE, None, ALU.mult)
                nc.vector.tensor_scalar(pw_sq[:], pw[:, 2:3], pw[:, 2:3], None, ALU.mult)
                link(nc.vector.reciprocal(pinv[:, 0:3], pw[:, 0:3]))
                nc.vector.tensor_scalar(o2_scale[:], pw_sq[:], pw[:, 2:3], 1.0 / (G_KEPT * W_SCALE),
                                        ALU.mult, ALU.mult)
                nc.vector.tensor_scalar(g_scale[:], pinv[:, 2:3], G_KEPT * H_TRUE, None, ALU.mult)
                nc.vector.tensor_scalar(wsc[:, 0:3], pinv[:, 0:3], W_SCALE, None, ALU.mult).then_inc(s_sc, 1)

                dve.wait_ge(s_sc, 1)
                for r in (0, 32):
                    nc.vector.tensor_scalar(row_tmp[r:r + 1, 0, :], bank[1][r:r + 1, 0:C], wsc[r:r + 1, 0:1], None,
                                            ALU.mult)
                    ins = nc.vector.tensor_scalar(row_tmp[r:r + 1, 1, :], bv_sb[r:r + 1, :], wsc[r:r + 1, 1:2], None,
                                                  ALU.mult)
                link(ins)
                nc.vector.tensor_copy(bias_rows[0:1, :, :], row_tmp[0:1, :, :])
                nc.vector.scalar_tensor_tensor(bias_rows[32:33, 0, :], bank[1][32:33, 0:C], wsc[32:33, 0:1],
                                               row_tmp[32:33, 0, :], ALU.mult, ALU.subtract)
                nc.vector.scalar_tensor_tensor(bias_rows[32:33, 1, :], bv_sb[32:33, :], wsc[32:33, 1:2],
                                               row_tmp[32:33, 1, :], ALU.mult, ALU.subtract).then_inc(s_wlo, 1)
                for k, (src, hi, lo) in enumerate(((bank[0], m_hi, m_lo), (bank[2], wv_hi, wv_lo))):
                    dve.wait_ge(s_whi, k + 1)
                    nc.vector.scalar_tensor_tensor(lo[:], src[:].rearrange("p (k c) -> p k c", k=KC),
                                                   wsc[:, k:k + 1], hi[:], ALU.mult, ALU.subtract).then_inc(s_wlo, 1)
                for r in range(B // 2):
                    dve.wait_ge(s_cThi, r + 1)
                    nc.vector.scalar_tensor_tensor(
                        cT_lo[:, 2 * r:2 * r + 2].rearrange("p b k f -> p (b k f)"), bank[4 + r % 4][:],
                        wsc[:, 2:3], cT_hi[:, 2 * r:2 * r + 2].rearrange("p b k f -> p (b k f)"),
                        ALU.mult, ALU.subtract).then_inc(s_cTlo, 1)
                dve.wait_ge(s_chi, 1)
                nc.vector.scalar_tensor_tensor(ctx_lo[:], ctx_sb[:], wsc[:, 2:3], ctx_hi[:], ALU.mult,
                                               ALU.subtract).then_inc(s_clo, 1)
                dve.wait_ge(s_ternc, 2)

            setup()

            def lo_transposed(k, b, banks):
                for kc in range(KC):
                    dve.wait_ge(xT_hi_ready[k], upto(b, KC, kc + 1))
                    nc.vector.tensor_tensor(xT_lo[k][:, kc, :], bank[banks[kc]][:], xT_hi[k][:, kc, :],
                                            ALU.subtract).then_inc(xT_ready[k], 1)

            def maxima(b, pair):
                for i in (2 * pair, 2 * pair + 1):
                    w = (i + 1) * P
                    dve.wait_ge(scores_psum, upto(b, NT, i + 1))
                    ins = nc.vector.tensor_reduce(negmax[:, i:i + 1], bank[4 + i % 2][:, 0:w], AX.X, ALU.max,
                                                  negate=True)
                ins.then_inc(max_ready, 1)
                dve.wait_ge(max_ready, upto(b, 2, pair + 1))
                nc.vector.tensor_scalar(ebias[:, 2 * pair:2 * pair + 2], negmax[:, 2 * pair:2 * pair + 2],
                                        exp_scale[:, 0:1], None, ALU.mult).then_inc(ebias_ready, 1)

            def prob_lo(b, tiles):
                for i in tiles:
                    w = (i + 1) * P
                    dve.wait_ge(pT_hi_ready, upto(b, NT, i + 1))
                    nc.vector.scalar_tensor_tensor(pT_lo[:, i, 0:w], bank[1 - i % 2][:, 0:w], P_SCALE,
                                                   pT_hi[:, i, 0:w], ALU.mult, ALU.subtract).then_inc(pT_ready, 1)

            def attended(b, parity, tiles):
                for i in tiles:
                    dve.wait_ge(att_psum, upto(b, NT, i + 1))
                    nc.vector.scalar_tensor_tensor(x2[:, i, :], bank[6 + i % 2][:, 0:C], oscale[:, i:i + 1],
                                                   xb[parity][:, i, :], ALU.mult, ALU.add).then_inc(x2_ready, 1)

            def body(n, parity, stages):
                if "A" in stages:
                    for kc in range(KC):
                        dve.wait_ge(q_hi_ready, upto(n, KC, kc + 1))
                        nc.vector.scalar_tensor_tensor(q_lo[:, kc, :], bank[2 + kc][:], QV_SCALE, q_hi[:, kc, :],
                                                       ALU.mult, ALU.subtract).then_inc(q_ready, 1)
                    for j in range(2):
                        dve.wait_ge(v_hi_ready, upto(n, 2, j + 1))
                        nc.vector.scalar_tensor_tensor(
                            v_lo[:, 2 * j:2 * j + 2, :], bank[4 + j][:].rearrange("p (i c) -> p i c", i=2), QV_SCALE,
                            v_hi[:, 2 * j:2 * j + 2, :], ALU.mult, ALU.subtract).then_inc(v_ready, 1)
                if "B" in stages:
                    lo_transposed(1, n - 1, (0, 1))
                if "C" in stages:
                    lo_transposed(2, n - 2, (6, 7))
                if "A" in stages:
                    maxima(n, 0)
                if "B" in stages:
                    dve.wait_ge(gelu_ready, upto(n - 1, 1, 1))
                    nc.vector.scalar_tensor_tensor(gbuf[:], bank[0][:], g_scale[:, 0:1], gel[:], ALU.mult,
                                                   ALU.mult).then_inc(g_ready, 1)
                if "C" in stages:
                    for j in range(2):
                        dve.wait_ge(had_psum, upto(n - 2, 2, j + 1))
                        ins = nc.vector.tensor_reduce(amax[:, 2 * j:2 * j + 2],
                                                      bank[2 + j][:].rearrange("p (i c) -> p i c", i=2), AX.X,
                                                      ALU.max, apply_absolute_value=True)
                    ins.then_inc(amax_ready, 1)
                    dve.wait_ge(amax_ready, upto(n - 2, 1, 1))
                    nc.vector.tensor_scalar(qs[:], amax[:], QUANT_MIN * HAD_SCALE, 1.0 / ACT_MAX, ALU.max,
                                            ALU.mult).then_inc(qs_ready, 1)
                    dve.wait_ge(qs_ready, upto(n - 2, 1, 1))
                    nc.vector.reciprocal(qinv[:], qs[:]).then_inc(qinv_ready, 1)
                if "B" in stages:
                    dve.wait_ge(g_hi_ready, upto(n - 1, 1, 1))
                    nc.vector.tensor_tensor(ghl[F:2 * F, :], gbuf[F:2 * F, :], ghl[F:2 * F, :], ALU.subtract)\
                        .then_inc(g_lo_ready, 1)
                if "A" in stages:
                    maxima(n, 1)
                if "Z" in stages:
                    dve.wait_ge(ld_x, upto(n + 1, 16, 16))
                    stats(0, n + 1, xb[1 - parity])
                if "A" in stages:
                    dve.wait_ge(prob_ready, upto(n, NT, NT))
                    nc.vector.reciprocal(prinv[:], psums[:]).then_inc(rinv_ready, 1)
                    prob_lo(n, (0, 1))
                    dve.wait_ge(rinv_ready, upto(n, 1, 1))
                    nc.vector.tensor_scalar(oscale[:], prinv[:], v_scale[:, 0:1], None, ALU.mult)\
                        .then_inc(oscale_ready, 1)
                if "B" in stages:
                    m_par = 1 - parity
                    if not (isinstance(n, int) and n < 3):
                        dve.wait_ge(st_y, upto(n - 3, 16, 16))
                    for i in range(NT):
                        dve.wait_ge(o2_psum, upto(n - 1, 2, i // 2 + 1))
                        nc.vector.scalar_tensor_tensor(x3[m_par][:, i, :],
                                                       bank[6 + i // 2][:, (i % 2) * C:(i % 2 + 1) * C],
                                                       o2_scale[:, 0:1], x2[:, i, :], ALU.mult, ALU.add)\
                            .then_inc(x3_ready, 1)
                if "A" in stages:
                    prob_lo(n, (2,))
                if "B" in stages:
                    dve.wait_ge(x3_ready, upto(n - 1, NT, NT))
                    stats(2, n - 1, x3[m_par])
                if "A" in stages:
                    dve.wait_ge(oscale_ready, upto(n, 1, 1))
                    attended(n, parity, (0, 1))
                if "C" in stages:
                    if not (isinstance(n, int) and n < 3):
                        dve.wait_ge(y_ready, upto(n - 3, 1, 1))
                    for i in range(NT):
                        dve.wait_ge(y_psum, upto(n - 2, 2, i // 2 + 1))
                        nc.vector.scalar_tensor_tensor(ytmp[:, i, :],
                                                       bank[2 + i // 2][:, (i % 2) * C:(i % 2 + 1) * C],
                                                       qs[:, i:i + 1], wsb[:], ALU.mult, ALU.mult)\
                            .then_inc(ytmp_ready, 1)
                if "A" in stages:
                    prob_lo(n, (3,))
                if "Z" in stages:
                    lo_transposed(0, n + 1, (4, 5))
                if "A" in stages:
                    attended(n, parity, (2, 3))
                    dve.wait_ge(x2_ready, upto(n, NT, NT))
                    stats(1, n, x2)

            steps(dve, body)

        @block.tensor
        def _(pe):
            mm = nc.tensor.matmul
            pe.wait_ge(ld_w, 16 * N_W)
            for kc in range(KC):
                for o in range(KC):
                    ins = mm(bank[0][:, kc * C:(kc + 1) * C], wq_sb[:, o, kc * P:(kc + 1) * P], wk_sb[:, o, :],
                             start=(o == 0), stop=(o == KC - 1))
            ins.then_inc(s_M, 1)
            pe.wait_ge(s_bqb, 1)
            for o in range(KC):
                ins = mm(bank[1][0:64, 0:C], bqb[:, o, :], wk_sb[:, o, :], start=(o == 0), stop=(o == KC - 1))
            ins.then_inc(s_w, 1)
            for kc in range(KC):
                for o in range(KC):
                    ins = nc.tensor.transpose(bank[2][:, kc * C + o * P:kc * C + (o + 1) * P],
                                              wv_sb[:, o, kc * P:(kc + 1) * P], idf[:])
            ins.then_inc(s_wvT, 1)
            pe.wait_ge(ld_ctx, 32)
            for r in range(B // 2):
                if r >= 4:
                    pe.wait_ge(s_cTlo, r - 3)
                for b in range(2):
                    for kc in range(KC):
                        ins = nc.tensor.transpose(bank[4 + r % 4][:, (b * KC + kc) * P:(b * KC + kc + 1) * P],
                                                  ctx_sb[:, 2 * r + b, kc * P:(kc + 1) * P], idf[:])
                ins.then_inc(s_cT, 1)
            pe.wait_ge(s_tern, 1)
            for kc in range(KC):
                for o in range(KC):
                    ins = nc.tensor.transpose(bank[3].bitcast(F16)[:, kc * C + o * P:kc * C + (o + 1) * P],
                                              tern[:, o, kc * P:(kc + 1) * P], idh[:])
            ins.then_inc(s_ternT, 1)
            pe.wait_ge(s_wlo, 1)
            for o in range(KC):
                ins = mm(bank[1][:, C + o * P:C + (o + 1) * P], ones[:], diag[:, o, :], start=True, stop=True)
            ins.then_inc(s_wsb, 1)
            pe.wait_ge(s_wlo, 3)
            pe.wait_ge(s_cTlo, B // 2)
            pe.wait_ge(s_clo, 1)
            pe.wait_ge(s_ternc, 2)

            def products(out, pairs, first=True, last=True):
                for j, (a, b) in enumerate(pairs):
                    ins = mm(out, a, b, start=(first and j == 0), stop=(last and j == len(pairs) - 1))
                return ins

            def transposes(k, b, banks):
                pe.wait_ge(xn_ready[k], upto(b, NT, NT))
                for kc in range(KC):
                    for i in range(NT):
                        ins = nc.tensor.transpose(bank[banks[kc]][:, i * P:(i + 1) * P],
                                                  xn[k][:, i, kc * P:(kc + 1) * P], idf[:])
                    ins.then_inc(xT_psum[k], 1)

            def query(n):
                for mc in range(KC):
                    cols = slice(mc * P, (mc + 1) * P)
                    pairs = [(bias_rows[:, 0, cols], one_rows[:])]
                    for kc in range(KC):
                        pairs += [(m_hi[:, kc, cols], xT_hi[0][:, kc, :]), (m_hi[:, kc, cols], xT_lo[0][:, kc, :]),
                                  (m_lo[:, kc, cols], xT_hi[0][:, kc, :])]
                    products(bank[2 + mc][:], pairs).then_inc(q_psum, 1)

            def value(n):
                for i in range(NT):
                    rows = slice(i * P, (i + 1) * P)
                    pairs = [(one_rows[:, 0:P], bias_rows[:, 1, :])]
                    for kc in range(KC):
                        pairs += [(xT_hi[0][:, kc, rows], wv_hi[:, kc, :]), (xT_hi[0][:, kc, rows], wv_lo[:, kc, :]),
                                  (xT_lo[0][:, kc, rows], wv_hi[:, kc, :])]
                    ins = products(bank[4 + i // 2][:, (i % 2) * C:(i % 2 + 1) * C], pairs)
                    if i % 2:
                        ins.then_inc(v_psum, 1)

            def scores(n, i):
                w = (i + 1) * P
                rows = slice(i * P, w)
                out = bank[4 + i % 2]
                pairs = []
                for kc in range(KC):
                    pairs += [(q_hi[:, kc, rows], xT_hi[0][:, kc, 0:w]), (q_hi[:, kc, rows], xT_lo[0][:, kc, 0:w]),
                              (q_lo[:, kc, rows], xT_hi[0][:, kc, 0:w])]
                products(out[:, 0:w], pairs, last=False)
                mm(out[:, rows], idh[:], msk[:], start=False, stop=True).then_inc(scores_psum, 1)

            def prob_transposes(n, i):
                pe.wait_ge(prob_ready, upto(n, NT, i + 1))
                for j in range(i + 1):
                    ins = nc.tensor.transpose(bank[1 - i % 2][:, j * P:(j + 1) * P], prob[:, i, j * P:(j + 1) * P],
                                              idf[:])
                ins.then_inc(pT_psum, 1)

            def attend(n, i):
                pe.wait_ge(pT_ready, upto(n, NT, i + 1))
                pairs = []
                for j in range(i + 1):
                    cols = slice(j * P, (j + 1) * P)
                    pairs += [(pT_hi[:, i, cols], v_hi[:, j, :]), (pT_hi[:, i, cols], v_lo[:, j, :]),
                              (pT_lo[:, i, cols], v_hi[:, j, :])]
                products(bank[6 + i % 2][:, 0:C], pairs).then_inc(att_psum, 1)

            def body(n, parity, stages):
                known = isinstance(n, int)
                if "A" in stages:
                    pe.wait_ge(xT_ready[0], upto(n, KC, KC))
                    if not (known and n < 3):
                        pe.wait_ge(ytmp_ready, upto(n - 3, NT, NT))
                    query(n)
                    value(n)
                if "B" in stages:
                    pe.wait_ge(pT_ready, upto(n - 1, NT, NT))
                    transposes(1, n - 1, (0, 1))
                if "C" in stages:
                    if known and n > B:
                        pe.wait_ge(x3_ready, upto(n - 2, NT, NT))
                    else:
                        pe.wait_ge(x2_ready, upto(n - 1, NT, NT))
                    transposes(2, n - 2, (6, 7))
                if "A" in stages:
                    pe.wait_ge(q_ready, upto(n, KC, KC))
                    for i in range(2):
                        pe.wait_ge(v_ready, upto(n, 2, i + 1))
                        scores(n, i)
                if "B" in stages:
                    pe.wait_ge(xT_ready[1], upto(n - 1, KC, KC))
                    m = n - 1
                    pairs = []
                    for kc in range(KC):
                        pairs += [(cT_hi[:, m, kc, :], xT_hi[1][:, kc, :]), (cT_hi[:, m, kc, :], xT_lo[1][:, kc, :]),
                                  (cT_lo[:, m, kc, :], xT_hi[1][:, kc, :])]
                    products(bank[0][:], pairs).then_inc(h_psum, 1)
                if "C" in stages:
                    pe.wait_ge(xT_ready[2], upto(n - 2, KC, KC))
                    if known and n >= B:
                        pe.wait_ge(ytmp_ready, upto(n - 3, NT, NT))
                    for i in range(NT):
                        rows = slice(i * P, (i + 1) * P)
                        pairs = []
                        for kc in range(KC):
                            pairs += [(xT_hi[2][:, kc, rows], had[:, kc, :]), (xT_lo[2][:, kc, rows], had[:, kc, :])]
                        ins = products(bank[2 + i // 2][:, (i % 2) * C:(i % 2 + 1) * C], pairs)
                        if i % 2:
                            ins.then_inc(had_psum, 1)
                if "A" in stages:
                    for i in (2, 3):
                        pe.wait_ge(prob_ready, upto(n, NT, i - 1))
                        scores(n, i)
                if "B" in stages:
                    if "C" not in stages:
                        pe.wait_ge(x2_ready, upto(n - 1, NT, NT))
                    pe.wait_ge(g_lo_ready, upto(n - 1, 1, 1))
                    for i in range(NT):
                        rows = slice(i * P, (i + 1) * P)
                        ins = products(bank[6 + i // 2][:, (i % 2) * C:(i % 2 + 1) * C],
                                       [(ghl[:, rows], ctx_hi[:, n - 1, :]), (ghl[:, rows], ctx_lo[:, n - 1, :])])
                        if i % 2:
                            ins.then_inc(o2_psum, 1)
                if "A" in stages:
                    prob_transposes(n, 0)
                    prob_transposes(n, 1)
                if "C" in stages:
                    pe.wait_ge(quant_ready, upto(n - 2, 1, 1))
                    for kc in range(KC):
                        for i in range(NT):
                            ins = nc.tensor.transpose(
                                bank[2].bitcast(F16)[:, kc * T + i * P:kc * T + (i + 1) * P],
                                quant[:, i, kc * P:(kc + 1) * P], idh[:])
                    ins.then_inc(qT_psum, 1)
                if "A" in stages:
                    pe.wait_ge(pT_ready, upto(n, NT, 1))
                    prob_transposes(n, 2)
                    for i in range(2):
                        if "B" in stages:
                            pe.wait_ge(x3_ready, upto(n - 1, NT, 2 * i + 2))
                        attend(n, i)
                if "C" in stages:
                    pe.wait_ge(qT_ready, upto(n - 2, 1, 1))
                    for i in range(NT):
                        rows = slice(i * P, (i + 1) * P)
                        ins = products(bank[2 + i // 2][:, (i % 2) * C:(i % 2 + 1) * C],
                                       [(qT[:, kc, rows], ternT[:, kc, :]) for kc in range(KC)])
                        if i % 2:
                            ins.then_inc(y_psum, 1)
                if "A" in stages:
                    pe.wait_ge(pT_ready, upto(n, NT, 2))
                    prob_transposes(n, 3)
                if "Z" in stages:
                    transposes(0, n + 1, (4, 5))
                if "A" in stages:
                    for i in (2, 3):
                        pe.wait_ge(x2_ready, upto(n, NT, i - 1))
                        attend(n, i)

            steps(pe, body)


def kernel(x, ctx_1024, L0_attn_Wq, L0_attn_bq, L0_attn_Wk, L0_attn_bk, L0_attn_Wv, L0_attn_bv, L0_ffn_weight):
    import concourse.bacc as bacc
    from concourse.bass_utils import run_bass_kernel_spmd

    C = x.shape[-1]
    signs = np.array([[1.0]])
    while signs.shape[0] < C:
        signs = np.block([[signs, signs], [signs, -signs]])
    later = np.triu(np.ones((P, P)), 1) * MASKED
    consts = {
        "hada": signs.astype(np.float16),
        "ident": np.eye(P, dtype=np.float32),
        "ident16": np.eye(P, dtype=np.float16),
        "mask": later.astype(mybir.dt.np(BF16)),
    }
    data = {
        "x": x, "ctx_kv": ctx_1024, "wq": L0_attn_Wq, "bq": np.reshape(L0_attn_bq, (-1, P)).T, "wk": L0_attn_Wk, "wv": L0_attn_Wv,
        "bv": L0_attn_bv, "wffn": L0_ffn_weight,
    }
    nc = bacc.Bacc("TRN2", target_bir_lowering=False, num_devices=1)
    arrays, aps = {}, {}
    for name, a in {**data, **consts}.items():
        a = np.ascontiguousarray(a)
        arrays[f"in_{name}"] = a
        aps[name] = nc.dram_tensor(f"in_{name}", a.shape, mybir.dt.from_np(a.dtype), kind="ExternalInput").ap()
    aps["y"] = nc.dram_tensor("out_y", x.shape, F32, kind="ExternalOutput").ap()
    build(nc, **aps)
    r = run_bass_kernel_spmd(nc, [arrays], core_ids=[0])
    return r.results[0]["out_y"]
```

```python
from contextlib import ExitStack

import numpy as np

import concourse.bass as bass
from concourse import mybir

F32 = mybir.dt.float32
F16 = mybir.dt.float16
BF16 = mybir.dt.bfloat16
I32 = mybir.dt.int32
ALU = mybir.AluOpType
ACT = mybir.ActivationFunctionType
AX = mybir.AxisListType

P = 128
LN_EPS = 1e-5
X_SCALE = 2.0 ** 8
XN_UP = 2.0 * X_SCALE
W_SCALE = 2.0 ** 13
QV_SCALE = 2.0 ** -15
P_SCALE = 2.0 ** 14
G_MIN = 2.0 ** -35
ROUND = 1.5 * 2.0 ** 23
MASKED = -1e30
ACT_MAX = 7.0
QUANT_MIN = 1e-5


def upto(batch, per_batch, k):
    return batch * per_batch + k


def build(nc, x, ctx_kv, wq, bq, wk, wv, bv, wffn, hada, ident, ident16, mask, y):
    B, T, C = x.shape
    F = ctx_kv.shape[1]
    NT = T // P
    KC = C // P
    assert (NT, KC, F) == (4, 2, 64) and B % 2 == 0 and B >= 6
    SM_SCALE = float(C) ** -0.5
    Q_SCALE2 = QV_SCALE * W_SCALE * X_SCALE
    S_EXP = SM_SCALE / (Q_SCALE2 * X_SCALE)
    H_TRUE = 1.0 / (W_SCALE * X_SCALE)
    G_KEPT = 2.0 ** -3
    H_DIM = float(C) ** 0.5
    HAD_SCALE = X_SCALE * H_DIM

    es = ExitStack()
    with es:
        def sb(name, shape, dt):
            return es.enter_context(nc.sbuf_tensor(name, shape, dt))

        def sem(name):
            return es.enter_context(nc.semaphore(name))

        bank = [es.enter_context(nc.psum_tensor(f"bank{i}", [P, 512], F32)) for i in range(8)]

        wq_sb = sb("wq_sb", [P, KC, C], F32)
        wk_sb = sb("wk_sb", [P, KC, C], F32)
        wv_sb = sb("wv_sb", [P, KC, C], F32)
        bq_sb = sb("bq_sb", [P, KC], F32)
        bv_sb = sb("bv_sb", [64, C], F32)
        wf_sb = sb("wf_sb", [P, KC, C], F32)
        ctx_sb = sb("ctx_sb", [P, B, C], F32)
        had = sb("had", [P, KC, C], F16)
        idf = sb("idf", [P, P], F32)
        idh = sb("idh", [P, P], F16)
        msk = sb("msk", [P, P], BF16)
        m_hi = sb("m_hi", [P, KC, C], F16)
        m_lo = sb("m_lo", [P, KC, C], F16)
        wv_hi = sb("wv_hi", [P, KC, C], F16)
        wv_lo = sb("wv_lo", [P, KC, C], F16)
        bias_rows = sb("bias_rows", [P, 2, C], F16)
        one_rows = sb("one_rows", [P, T], F16)
        ctx_hi = sb("ctx_hi", [P, B, C], F16)
        ctx_lo = sb("ctx_lo", [P, B, C], F16)
        cT_hi = sb("cT_hi", [P, B, KC, P], F16)
        cT_lo = sb("cT_lo", [P, B, KC, P], F16)
        ternT = sb("ternT", [P, KC, C], F16)
        wsb = sb("wsb", [P, C], F32)
        ones = sb("ones", [P, P], F32)
        bqb = sb("bqb", [P, KC, 64], F32)
        red = sb("red", [P, 4], F32)
        redw = sb("redw", [P, 4], F32)
        gmax = sb("gmax", [P, 4], F32)
        pw = sb("pw", [P, 4], F32)
        pinv = sb("pinv", [P, 4], F32)
        wsc = sb("wsc", [P, 4], F32)
        row_tmp = sb("row_tmp", [64, 2, C], F16)
        wsum = sb("wsum", [P, KC], F32)
        wmean = sb("wmean", [P, KC], F32)
        thr = sb("thr", [P, 2, KC], F32)
        tern_p = sb("tern_p", [P, KC, C], F32)
        tern_n = sb("tern_n", [P, KC, C], F32)
        tern = sb("tern", [P, KC, C], F16)
        diag = sb("diag", [P, KC, P], F32)
        pw_sq = sb("pw_sq", [P, 1], F32)
        exp_scale = sb("exp_scale", [P, 1], F32)
        v_scale = sb("v_scale", [P, 1], F32)
        h_scale = sb("h_scale", [P, 1], F32)
        g_scale = sb("g_scale", [P, 1], F32)
        o2_scale = sb("o2_scale", [P, 1], F32)
        rnd = sb("rnd", [P, 1], F32)
        unrnd = sb("unrnd", [P, 1], F32)
        mhalf = sb("mhalf", [P, NT], F32)

        xb = [sb(f"x_{i}", [P, NT, C], F32) for i in range(2)]
        x2 = [sb(f"x2_{i}", [P, NT, C], F32) for i in range(2)]
        x3 = [sb(f"x3_{i}", [P, NT, C], F32) for i in range(2)]
        ytmp = sb("ytmp", [P, NT, C], F32)
        xn = [sb(f"xn_{i}", [P, NT, C], F32) for i in range(3)]
        xT_hi = [sb(f"xT_hi_{i}", [P, KC, T], F16) for i in range(3)]
        xT_lo = [sb(f"xT_lo_{i}", [P, KC, T], F16) for i in range(3)]
        st = [sb(f"st_{i}", [P, NT, 6], F32) for i in range(3)]
        msum = sb("msum", [P, NT], F32)
        mdif = sb("mdif", [P, NT], F32)
        dev = sb("dev", [P, NT], F32)
        dev4 = sb("dev4", [P, NT], F32)
        mdif2 = sb("mdif2", [P, NT], F32)
        nmean = sb("nmean", [P, NT], F32)
        var4 = sb("var4", [P, NT], F32)
        rstd = sb("rstd", [P, NT], F32)
        q_hi = sb("q_hi", [P, KC, T], F16)
        q_lo = sb("q_lo", [P, KC, T], F16)
        v_hi = sb("v_hi", [P, NT, C], F16)
        v_lo = sb("v_lo", [P, NT, C], F16)
        negmax = sb("negmax", [P, NT], F32)
        ebias = sb("ebias", [P, NT], F32)
        prob = sb("prob", [P, NT, T], F32)
        psums = sb("psums", [P, NT], F32)
        prinv = sb("prinv", [P, NT], F32)
        oscale = sb("oscale", [P, NT], F32)
        pT_hi = sb("pT_hi", [P, NT, T], F16)
        pT_lo = sb("pT_lo", [P, NT, T], F16)
        gel = sb("gel", [P, T], F32)
        gbuf = sb("gbuf", [P, T], F32)
        ghl = sb("ghl", [P, T], F16)
        amax = sb("amax", [P, NT], F32)
        qs = sb("qs", [P, NT], F32)
        qinv = sb("qinv", [P, NT], F32)
        rounded = sb("rounded", [P, NT, C], F32)
        quant = sb("quant", [P, NT, C], F16)
        qT = sb("qT", [P, KC, T], F16)

        ld_w = sem("ld_w")
        ld_ctx = sem("ld_ctx")
        ld_x = sem("ld_x")
        st_y = sem("st_y")
        s_ones = sem("s_ones")
        s_bqb = sem("s_bqb")
        s_M = sem("s_M")
        s_w = sem("s_w")
        s_wvT = sem("s_wvT")
        s_red = sem("s_red")
        s_all = sem("s_all")
        s_sc = sem("s_sc")
        s_whi = sem("s_whi")
        s_wlo = sem("s_wlo")
        s_chi = sem("s_chi")
        s_clo = sem("s_clo")
        s_cT = sem("s_cT")
        s_cThi = sem("s_cThi")
        s_cTlo = sem("s_cTlo")
        s_tern = sem("s_tern")
        s_ternT = sem("s_ternT")
        s_ternc = sem("s_ternc")
        s_diag = sem("s_diag")
        s_wsb = sem("s_wsb")
        s_wsc = sem("s_wsc")
        s_dv = sem("s_dv")
        stats_ready = [sem(f"stats_ready_{i}") for i in range(3)]
        xn_ready = [sem(f"xn_ready_{i}") for i in range(3)]
        xT_psum = [sem(f"xT_psum_{i}") for i in range(3)]
        xT_hi_ready = [sem(f"xT_hi_ready_{i}") for i in range(3)]
        xT_ready = [sem(f"xT_ready_{i}") for i in range(3)]
        q_psum = sem("q_psum")
        q_hi_ready = sem("q_hi_ready")
        q_ready = sem("q_ready")
        v_psum = sem("v_psum")
        v_hi_ready = sem("v_hi_ready")
        v_ready = sem("v_ready")
        scores_psum = sem("scores_psum")
        max_ready = sem("max_ready")
        ebias_ready = sem("ebias_ready")
        prob_ready = sem("prob_ready")
        pT_psum = sem("pT_psum")
        pT_hi_ready = sem("pT_hi_ready")
        pT_ready = sem("pT_ready")
        rinv_ready = sem("rinv_ready")
        oscale_ready = sem("oscale_ready")
        att_psum = sem("att_psum")
        x2_ready = sem("x2_ready")
        h_psum = sem("h_psum")
        gelu_ready = sem("gelu_ready")
        g_ready = sem("g_ready")
        g_hi_ready = sem("g_hi_ready")
        g_lo_ready = sem("g_lo_ready")
        o2_psum = sem("o2_psum")
        x3_ready = sem("x3_ready")
        had_psum = sem("had_psum")
        amax_ready = sem("amax_ready")
        qs_ready = sem("qs_ready")
        qinv_ready = sem("qinv_ready")
        round_ready = sem("round_ready")
        quant_ready = sem("quant_ready")
        qT_psum = sem("qT_psum")
        qT_ready = sem("qT_ready")
        y_psum = sem("y_psum")
        ytmp_ready = sem("ytmp_ready")
        y_ready = sem("y_ready")

        x_v = x.rearrange("b (i p) c -> b p i c", p=P)
        y_v = y.rearrange("b (i p) c -> b p i c", p=P)
        N_W = 11

        def steps(eng, body):
            body(-1, 1, "Z")
            body(0, 0, "ZA")
            body(1, 1, "ZAB")
            body(2, 0, "ZABC")
            body(3, 1, "ZABCD")
            with eng.Fori(2, B // 2 - 1) as pair:
                body(pair * 2, 0, "ZABCD")
                body(pair * 2 + 1, 1, "ZABCD")
            body(B - 2, 0, "ZABCD")
            body(B - 1, 1, "ABCD")
            body(B, 0, "BCD")
            body(B + 1, 1, "CD")
            body(B + 2, 0, "D")

        block = es.enter_context(nc.Block())

        @block.sync
        def _(sp):
            def load_x(b, parity):
                sp.dma_start(xb[parity][:], x_v[b]).then_inc(ld_x, 16)

            load_x(0, 0)
            sp.dma_start(idf[:], ident).then_inc(ld_w, 16)
            sp.dma_start(wq_sb[:], wq.rearrange("(k p) c -> p k c", p=P)).then_inc(ld_w, 16)
            sp.dma_start(wk_sb[:], wk.rearrange("(k p) c -> p k c", p=P)).then_inc(ld_w, 16)
            sp.dma_start(bq_sb[:], bq).then_inc(ld_w, 16)
            sp.dma_start(wv_sb[:], wv.rearrange("(k p) c -> p k c", p=P)).then_inc(ld_w, 16)
            for r in (0, 32):
                sp.dma_start(bv_sb[r:r + 1, :], bv.rearrange("(a c) -> a c", a=1)).then_inc(ld_w, 16)
            sp.dma_start(wf_sb[:], wffn.rearrange("(k p) c -> p k c", p=P)).then_inc(ld_w, 16)
            sp.dma_start(had[:], hada.rearrange("(k p) c -> p k c", p=P)).then_inc(ld_w, 16)
            sp.dma_start(idh[:], ident16).then_inc(ld_w, 16)
            sp.dma_start(msk[:], mask).then_inc(ld_w, 16)

            def body(n, parity, stages):
                if "D" in stages:
                    sp.wait_ge(y_ready, upto(n - 3, 1, 1))
                    sp.dma_start(y_v[n - 3], x3[1 - parity][:]).then_inc(st_y, 16)
                if stages == "Z":
                    sp.wait_ge(ld_x, 16)
                    load_x(1, 1)
                elif "A" in stages and "Z" in stages:
                    if isinstance(n, int) and n + 2 >= B:
                        return
                    sp.wait_ge(x2_ready, upto(n, NT, NT))
                    load_x(n + 2, parity)

            steps(sp, body)
            sp.wait_ge(st_y, 16 * B)

        @block.gpsimd
        def _(pool):
            nc.gpsimd.memset(ones[:], 1.0)
            nc.gpsimd.memset(rnd[:], ROUND)
            nc.gpsimd.memset(unrnd[:], -ROUND)
            nc.gpsimd.memset(mhalf[:], -0.5)
            nc.gpsimd.memset(bias_rows[:], 0.0)
            nc.gpsimd.memset(one_rows[:], 0.0).then_inc(s_ones, 1)
            for h in range(2):
                nc.gpsimd.dma_start(ctx_sb[h * F:(h + 1) * F], ctx_kv.rearrange("b f c -> f b c"))\
                    .then_inc(ld_ctx, 16)
            pool.wait_ge(s_ones, 1)
            nc.gpsimd.memset(one_rows[0:1, :], X_SCALE)
            nc.gpsimd.memset(one_rows[32:33, :], X_SCALE).then_inc(s_ones, 1)
            pool.wait_ge(s_ones, 2)
            pool.wait_ge(s_red, 1)
            nc.gpsimd.partition_all_reduce(gmax[:, 0:3], red[:, 0:3], P, bass.bass_isa.ReduceOp.max)\
                .then_inc(s_all, 1)

            def normalise(k, b, src):
                mean_e, dev_e, mean_o, dev_o = (st[k][:, :, j] for j in (1, 2, 4, 5))
                pool.wait_ge(stats_ready[k], upto(b, 1, 1))
                nc.gpsimd.tensor_tensor(msum[:], mean_e, mean_o, ALU.add)
                nc.gpsimd.tensor_tensor(mdif[:], mean_e, mean_o, ALU.subtract)
                nc.gpsimd.tensor_tensor(dev[:], dev_e, dev_o, ALU.add)
                pool.drain()
                nc.gpsimd.tensor_scalar(dev4[:], dev[:], 4.0 / C, 4.0 * LN_EPS, ALU.mult, ALU.add)
                nc.gpsimd.tensor_tensor(mdif2[:], mdif[:], mdif[:], ALU.mult)
                nc.gpsimd.tensor_tensor(nmean[:], msum[:], mhalf[:], ALU.mult)
                pool.drain()
                nc.gpsimd.tensor_tensor(var4[:], dev4[:], mdif2[:], ALU.add)
                pool.drain()
                nc.gpsimd.tensor_tensor(rstd[:], var4[:], mhalf[:], ALU.pow)
                pool.drain()
                for i in range(NT):
                    nc.gpsimd.tensor_scalar(xn[k][:, i, :], src[:, i, :], nmean[:, i:i + 1], rstd[:, i:i + 1],
                                            ALU.add, ALU.mult).then_inc(xn_ready[k], 1)

            def body(n, parity, stages):
                if "B" in stages:
                    normalise(1, n - 1, x2[1 - parity])
                if "Z" in stages:
                    normalise(0, n + 1, xb[1 - parity])
                if "C" in stages:
                    normalise(2, n - 2, x3[parity])
                if "D" in stages:
                    pool.wait_ge(ytmp_ready, upto(n - 3, NT, NT))
                    nc.gpsimd.tensor_tensor(x3[1 - parity][:], x3[1 - parity][:], ytmp[:], ALU.add)\
                        .then_inc(y_ready, 1)

            steps(pool, body)

        @block.scalar
        def _(act):
            act.wait_ge(s_sc, 1)
            nc.scalar.activation(m_hi[:], bank[0][:].rearrange("p (k c) -> p k c", k=KC), ACT.Copy,
                                 scale=wsc[:, 0:1]).then_inc(s_whi, 1)
            act.wait_ge(s_wvT, 1)
            nc.scalar.activation(wv_hi[:], bank[2][:].rearrange("p (k c) -> p k c", k=KC), ACT.Copy,
                                 scale=wsc[:, 1:2]).then_inc(s_whi, 1)
            for r in range(B // 2):
                act.wait_ge(s_cT, r + 1)
                nc.scalar.activation(cT_hi[:, 2 * r:2 * r + 2],
                                     bank[4 + r % 4][:].rearrange("p (b k f) -> p b k f", b=2, k=KC),
                                     ACT.Copy, scale=wsc[:, 2:3]).then_inc(s_cThi, 1)
            nc.scalar.activation(ctx_hi[:], ctx_sb[:], ACT.Copy, scale=wsc[:, 2:3]).then_inc(s_chi, 1)
            act.wait_ge(s_ternT, 1)
            nc.scalar.activation(ternT[:], bank[3].bitcast(F16)[:, 0:512].rearrange("p (k c) -> p k c", k=KC),
                                 ACT.Copy).then_inc(s_ternc, 1)
            act.wait_ge(s_wsb, 1)
            nc.scalar.activation(wsb[:], bank[1][:, 256:512], ACT.Copy, scale=1.0 / HAD_SCALE)\
                .then_inc(s_ternc, 1)
            act.wait_ge(s_ones, 2)

            def hi_transposed(k, b, banks):
                for kc in range(KC):
                    act.wait_ge(xT_psum[k], upto(b, KC, kc + 1))
                    nc.scalar.activation(xT_hi[k][:, kc, :], bank[banks[kc]][:], ACT.Copy, scale=XN_UP)\
                        .then_inc(xT_hi_ready[k], 1)

            def exps(b, tiles):
                for i in tiles:
                    w = (i + 1) * P
                    act.wait_ge(ebias_ready, upto(b, 2, i // 2 + 1))
                    nc.scalar.activation(prob[:, i, 0:w], bank[2 + i][:, 0:w], ACT.Exp,
                                         bias=ebias[:, i:i + 1], scale=exp_scale[:, 0:1],
                                         accum_out=psums[:, i:i + 1]).then_inc(prob_ready, 1)

            def prob_hi(b, tiles):
                for i in tiles:
                    w = (i + 1) * P
                    act.wait_ge(pT_psum, upto(b, NT, i + 1))
                    nc.scalar.activation(pT_hi[:, i, 0:w], bank[2 + i][:, 0:w], ACT.Copy,
                                         scale=P_SCALE).then_inc(pT_hi_ready, 1)

            def query_hi(b):
                for kc in range(KC):
                    act.wait_ge(q_psum, upto(b, KC, kc + 1))
                    nc.scalar.activation(q_hi[:, kc, :], bank[2 + kc][:], ACT.Copy, scale=QV_SCALE)\
                        .then_inc(q_hi_ready, 1)

            def value_hi(b, j):
                act.wait_ge(v_psum, upto(b, 2, j + 1))
                nc.scalar.activation(v_hi[:, 2 * j:2 * j + 2, :], bank[4 + j][:].rearrange("p (i c) -> p i c", i=2),
                                     ACT.Copy, scale=QV_SCALE).then_inc(v_hi_ready, 1)

            def body(n, parity, stages):
                if "A" in stages:
                    query_hi(n)
                if "D" in stages:
                    act.wait_ge(qinv_ready, upto(n - 3, 1, 1))
                    for i in range(NT):
                        nc.scalar.activation(rounded[:, i, :], bank[i // 2][:, (i % 2) * C:(i % 2 + 1) * C],
                                             ACT.Identity, bias=rnd[:, 0:1], scale=qinv[:, i:i + 1])\
                            .then_inc(round_ready, 1)
                if "A" in stages:
                    value_hi(n, 0)
                if "D" in stages:
                    act.wait_ge(round_ready, upto(n - 3, NT, NT))
                    nc.scalar.activation(quant[:], rounded[:], ACT.Identity, bias=unrnd[:, 0:1])\
                        .then_inc(quant_ready, 1)
                if "A" in stages:
                    value_hi(n, 1)
                    exps(n, (0, 1))
                if "D" in stages:
                    act.wait_ge(qT_psum, upto(n - 3, 1, 1))
                    nc.scalar.activation(qT[:], bank[0].bitcast(F16)[:, :].rearrange("p (k t) -> p k t", k=KC),
                                         ACT.Copy).then_inc(qT_ready, 1)
                if "B" in stages:
                    hi_transposed(1, n - 1, (6, 7))
                if "A" in stages:
                    prob_hi(n, (0, 1))
                    exps(n, (2, 3))
                if "Z" in stages:
                    hi_transposed(0, n + 1, (0, 1))
                if "A" in stages:
                    prob_hi(n, (2, 3))
                if "B" in stages:
                    act.wait_ge(h_psum, upto(n - 1, 1, 1))
                    nc.scalar.activation(gel[:], bank[6][:], ACT.Gelu, scale=h_scale[:, 0:1])\
                        .then_inc(gelu_ready, 1)
                if "C" in stages:
                    hi_transposed(2, n - 2, (0, 1))
                if "B" in stages:
                    act.wait_ge(g_ready, upto(n - 1, 1, 1))
                    nc.scalar.activation(ghl[:], gbuf[:], ACT.Copy).then_inc(g_hi_ready, 1)

            steps(act, body)

        @block.vector
        def _(dve):
            done = [0]

            def link(ins):
                done[0] += 1
                ins.then_inc(s_dv, 1)
                dve.wait_ge(s_dv, done[0])

            dve.wait_ge(ld_w, 16 * N_W)
            dve.wait_ge(s_ones, 2)
            for k in range(KC):
                ins = nc.vector.tensor_scalar(bqb[:, k, :], ones[:, 0:64], bq_sb[:, k:k + 1], None, ALU.mult)
            ins.then_inc(s_bqb, 1)

            def stats(k, b, src):
                for i in range(NT):
                    ins = nc.vector.bn_stats(st[k][:, i, :], src[:, i, :])
                ins.then_inc(stats_ready[k], 1)

            def setup():
                nc.vector.tensor_reduce(wsum[:], wf_sb[:], AX.X, ALU.add, apply_absolute_value=True)
                nc.vector.tensor_reduce(red[:, 1:2], wv_sb[:], AX.XY, ALU.max, apply_absolute_value=True)
                link(nc.vector.tensor_reduce(redw[0:1, 1:2], bv_sb[0:1, :], AX.X, ALU.max,
                                             apply_absolute_value=True))
                nc.vector.tensor_tensor(red[0:1, 1:2], red[0:1, 1:2], redw[0:1, 1:2], ALU.max)
                link(nc.vector.tensor_scalar(wmean[:], wsum[:], 1.0 / C, QUANT_MIN, ALU.mult, ALU.max))
                nc.vector.tensor_scalar(thr[:, 0, :], wmean[:], 0.5, None, ALU.mult)
                link(nc.vector.tensor_scalar(thr[:, 1, :], wmean[:], -0.5, None, ALU.mult))
                for k in range(KC):
                    nc.vector.tensor_scalar(diag[:, k, :], idf[:], wmean[:, k:k + 1], None, ALU.mult)
                    nc.vector.tensor_scalar(tern_p[:, k, :], wf_sb[:, k, :], thr[:, 0, k:k + 1], None, ALU.is_gt)
                    ins = nc.vector.tensor_scalar(tern_n[:, k, :], wf_sb[:, k, :], thr[:, 1, k:k + 1], None,
                                                  ALU.is_lt)
                link(ins)
                link(nc.vector.tensor_tensor(tern[:], tern_p[:], tern_n[:], ALU.subtract))
                nc.vector.engine_nop().then_inc(s_tern, 1)

                dve.wait_ge(s_w, 1)
                nc.vector.tensor_reduce(red[:, 0:1], bank[0][:], AX.X, ALU.max, apply_absolute_value=True)
                link(nc.vector.tensor_reduce(redw[0:64, 0:1], bank[1][0:64, 0:C], AX.X, ALU.max,
                                             apply_absolute_value=True))
                nc.vector.tensor_tensor(red[0:64, 0:1], red[0:64, 0:1], redw[0:64, 0:1], ALU.max)
                dve.wait_ge(ld_ctx, 32)
                nc.vector.tensor_reduce(red[:, 2:3], ctx_sb[:], AX.XY, ALU.max, apply_absolute_value=True)\
                    .then_inc(s_red, 1)

                dve.wait_ge(s_all, 1)
                link(nc.vector.tensor_scalar(gmax[:, 0:3], gmax[:, 0:3], G_MIN, None, ALU.max))
                link(nc.vector.tensor_scalar(pw[:, 0:3].bitcast(I32), gmax[:, 0:3].bitcast(I32), 0x7F800000, None,
                                             ALU.bitwise_and))
                nc.vector.tensor_scalar(exp_scale[:], pw[:, 0:1], S_EXP, None, ALU.mult)
                nc.vector.tensor_scalar(v_scale[:], pw[:, 1:2], 1.0 / (P_SCALE * Q_SCALE2), None, ALU.mult)
                nc.vector.tensor_scalar(h_scale[:], pw[:, 2:3], H_TRUE, None, ALU.mult)
                nc.vector.tensor_scalar(pw_sq[:], pw[:, 2:3], pw[:, 2:3], None, ALU.mult)
                link(nc.vector.reciprocal(pinv[:, 0:3], pw[:, 0:3]))
                nc.vector.tensor_scalar(o2_scale[:], pw_sq[:], pw[:, 2:3], 1.0 / (G_KEPT * W_SCALE),
                                        ALU.mult, ALU.mult)
                nc.vector.tensor_scalar(g_scale[:], pinv[:, 2:3], G_KEPT * H_TRUE, None, ALU.mult)
                nc.vector.tensor_scalar(wsc[:, 0:3], pinv[:, 0:3], W_SCALE, None, ALU.mult).then_inc(s_sc, 1)

                dve.wait_ge(s_sc, 1)
                for r in (0, 32):
                    nc.vector.tensor_scalar(row_tmp[r:r + 1, 0, :], bank[1][r:r + 1, 0:C], wsc[r:r + 1, 0:1], None,
                                            ALU.mult)
                    ins = nc.vector.tensor_scalar(row_tmp[r:r + 1, 1, :], bv_sb[r:r + 1, :], wsc[r:r + 1, 1:2], None,
                                                  ALU.mult)
                link(ins)
                nc.vector.tensor_copy(bias_rows[0:1, :, :], row_tmp[0:1, :, :])
                nc.vector.scalar_tensor_tensor(bias_rows[32:33, 0, :], bank[1][32:33, 0:C], wsc[32:33, 0:1],
                                               row_tmp[32:33, 0, :], ALU.mult, ALU.subtract)
                nc.vector.scalar_tensor_tensor(bias_rows[32:33, 1, :], bv_sb[32:33, :], wsc[32:33, 1:2],
                                               row_tmp[32:33, 1, :], ALU.mult, ALU.subtract).then_inc(s_wlo, 1)
                for k, (src, hi, lo) in enumerate(((bank[0], m_hi, m_lo), (bank[2], wv_hi, wv_lo))):
                    dve.wait_ge(s_whi, k + 1)
                    nc.vector.scalar_tensor_tensor(lo[:], src[:].rearrange("p (k c) -> p k c", k=KC),
                                                   wsc[:, k:k + 1], hi[:], ALU.mult, ALU.subtract).then_inc(s_wlo, 1)
                for r in range(B // 2):
                    dve.wait_ge(s_cThi, r + 1)
                    nc.vector.scalar_tensor_tensor(
                        cT_lo[:, 2 * r:2 * r + 2].rearrange("p b k f -> p (b k f)"), bank[4 + r % 4][:],
                        wsc[:, 2:3], cT_hi[:, 2 * r:2 * r + 2].rearrange("p b k f -> p (b k f)"),
                        ALU.mult, ALU.subtract).then_inc(s_cTlo, 1)
                dve.wait_ge(s_chi, 1)
                nc.vector.scalar_tensor_tensor(ctx_lo[:], ctx_sb[:], wsc[:, 2:3], ctx_hi[:], ALU.mult,
                                               ALU.subtract).then_inc(s_clo, 1)
                dve.wait_ge(s_ternc, 2)

            setup()

            def lo_transposed(k, b, banks):
                for kc in range(KC):
                    dve.wait_ge(xT_hi_ready[k], upto(b, KC, kc + 1))
                    nc.vector.scalar_tensor_tensor(xT_lo[k][:, kc, :], bank[banks[kc]][:], XN_UP, xT_hi[k][:, kc, :],
                                                   ALU.mult, ALU.subtract).then_inc(xT_ready[k], 1)

            def maxima(b, pair):
                for i in (2 * pair, 2 * pair + 1):
                    w = (i + 1) * P
                    dve.wait_ge(scores_psum, upto(b, NT, i + 1))
                    ins = nc.vector.tensor_reduce(negmax[:, i:i + 1], bank[2 + i][:, 0:w], AX.X, ALU.max,
                                                  negate=True)
                ins.then_inc(max_ready, 1)
                dve.wait_ge(max_ready, upto(b, 2, pair + 1))
                nc.vector.tensor_scalar(ebias[:, 2 * pair:2 * pair + 2], negmax[:, 2 * pair:2 * pair + 2],
                                        exp_scale[:, 0:1], None, ALU.mult).then_inc(ebias_ready, 1)

            def prob_lo(b, tiles):
                for i in tiles:
                    w = (i + 1) * P
                    dve.wait_ge(pT_hi_ready, upto(b, NT, i + 1))
                    nc.vector.scalar_tensor_tensor(pT_lo[:, i, 0:w], bank[2 + i][:, 0:w], P_SCALE,
                                                   pT_hi[:, i, 0:w], ALU.mult, ALU.subtract).then_inc(pT_ready, 1)

            def attended(b, parity, tiles):
                for i in tiles:
                    dve.wait_ge(att_psum, upto(b, NT, i + 1))
                    nc.vector.scalar_tensor_tensor(x2[parity][:, i, :], bank[2 + i][:, 0:C], oscale[:, i:i + 1],
                                                   xb[parity][:, i, :], ALU.mult, ALU.add).then_inc(x2_ready, 1)

            def query_lo(b):
                for kc in range(KC):
                    dve.wait_ge(q_hi_ready, upto(b, KC, kc + 1))
                    nc.vector.scalar_tensor_tensor(q_lo[:, kc, :], bank[2 + kc][:], QV_SCALE, q_hi[:, kc, :],
                                                   ALU.mult, ALU.subtract).then_inc(q_ready, 1)

            def value_lo(b, j):
                dve.wait_ge(v_hi_ready, upto(b, 2, j + 1))
                nc.vector.scalar_tensor_tensor(
                    v_lo[:, 2 * j:2 * j + 2, :], bank[4 + j][:].rearrange("p (i c) -> p i c", i=2), QV_SCALE,
                    v_hi[:, 2 * j:2 * j + 2, :], ALU.mult, ALU.subtract).then_inc(v_ready, 1)

            def quant_scale(b):
                for j in range(2):
                    dve.wait_ge(had_psum, upto(b, 2, j + 1))
                    ins = nc.vector.tensor_reduce(amax[:, 2 * j:2 * j + 2],
                                                  bank[j][:].rearrange("p (i c) -> p i c", i=2), AX.X, ALU.max,
                                                  apply_absolute_value=True)
                ins.then_inc(amax_ready, 1)
                dve.wait_ge(amax_ready, upto(b, 1, 1))
                nc.vector.tensor_scalar(qs[:], amax[:], QUANT_MIN * HAD_SCALE, 1.0 / ACT_MAX, ALU.max, ALU.mult)\
                    .then_inc(qs_ready, 1)
                dve.wait_ge(qs_ready, upto(b, 1, 1))
                nc.vector.reciprocal(qinv[:], qs[:]).then_inc(qinv_ready, 1)

            def cross_attended(b, parity):
                for i in range(NT):
                    dve.wait_ge(o2_psum, upto(b, 2, i // 2 + 1))
                    nc.vector.scalar_tensor_tensor(x3[parity][:, i, :],
                                                   bank[6 + i // 2][:, (i % 2) * C:(i % 2 + 1) * C],
                                                   o2_scale[:, 0:1], x2[parity][:, i, :], ALU.mult, ALU.add)\
                        .then_inc(x3_ready, 1)

            def ffn_scaled(b, j):
                dve.wait_ge(y_psum, upto(b, 2, j + 1))
                for i in (2 * j, 2 * j + 1):
                    nc.vector.scalar_tensor_tensor(ytmp[:, i, :], bank[6 + j][:, (i % 2) * C:(i % 2 + 1) * C],
                                                   qs[:, i:i + 1], wsb[:], ALU.mult, ALU.mult)\
                        .then_inc(ytmp_ready, 1)

            def body(n, parity, stages):
                known = isinstance(n, int)
                if "A" in stages:
                    query_lo(n)
                if "D" in stages:
                    quant_scale(n - 3)
                if "Z" in stages:
                    dve.wait_ge(ld_x, upto(n + 1, 16, 16))
                    stats(0, n + 1, xb[1 - parity])
                if "C" in stages:
                    if not (known and n < 4):
                        dve.wait_ge(st_y, upto(n - 4, 16, 16))
                    cross_attended(n - 2, parity)
                if "A" in stages:
                    value_lo(n, 0)
                    maxima(n, 0)
                    value_lo(n, 1)
                if "C" in stages:
                    dve.wait_ge(x3_ready, upto(n - 2, NT, NT))
                    stats(2, n - 2, x3[parity])
                if "A" in stages:
                    maxima(n, 1)
                if "B" in stages:
                    lo_transposed(1, n - 1, (6, 7))
                if "A" in stages:
                    prob_lo(n, (0, 1))
                if "D" in stages:
                    if not (known and n < 4):
                        dve.wait_ge(y_ready, upto(n - 4, 1, 1))
                    ffn_scaled(n - 3, 0)
                if "A" in stages:
                    dve.wait_ge(prob_ready, upto(n, NT, NT))
                    nc.vector.reciprocal(prinv[:], psums[:]).then_inc(rinv_ready, 1)
                if "D" in stages:
                    ffn_scaled(n - 3, 1)
                if "A" in stages:
                    dve.wait_ge(rinv_ready, upto(n, 1, 1))
                    nc.vector.tensor_scalar(oscale[:], prinv[:], v_scale[:, 0:1], None, ALU.mult)\
                        .then_inc(oscale_ready, 1)
                if "Z" in stages:
                    lo_transposed(0, n + 1, (0, 1))
                if "A" in stages:
                    prob_lo(n, (2,))
                    dve.wait_ge(oscale_ready, upto(n, 1, 1))
                    attended(n, parity, (0, 1))
                    prob_lo(n, (3,))
                if "B" in stages:
                    dve.wait_ge(gelu_ready, upto(n - 1, 1, 1))
                    nc.vector.scalar_tensor_tensor(gbuf[:], bank[6][:], g_scale[:, 0:1], gel[:], ALU.mult,
                                                   ALU.mult).then_inc(g_ready, 1)
                if "C" in stages:
                    lo_transposed(2, n - 2, (0, 1))
                if "A" in stages:
                    attended(n, parity, (2, 3))
                if "B" in stages:
                    dve.wait_ge(g_hi_ready, upto(n - 1, 1, 1))
                    nc.vector.tensor_tensor(ghl[F:2 * F, :], gbuf[F:2 * F, :], ghl[F:2 * F, :], ALU.subtract)\
                        .then_inc(g_lo_ready, 1)
                if "A" in stages:
                    dve.wait_ge(x2_ready, upto(n, NT, NT))
                    stats(1, n, x2[parity])

            steps(dve, body)

        @block.tensor
        def _(pe):
            mm = nc.tensor.matmul
            pe.wait_ge(ld_w, 16 * N_W)
            for kc in range(KC):
                for o in range(KC):
                    ins = mm(bank[0][:, kc * C:(kc + 1) * C], wq_sb[:, o, kc * P:(kc + 1) * P], wk_sb[:, o, :],
                             start=(o == 0), stop=(o == KC - 1))
            ins.then_inc(s_M, 1)
            pe.wait_ge(s_bqb, 1)
            for o in range(KC):
                ins = mm(bank[1][0:64, 0:C], bqb[:, o, :], wk_sb[:, o, :], start=(o == 0), stop=(o == KC - 1))
            ins.then_inc(s_w, 1)
            for kc in range(KC):
                for o in range(KC):
                    ins = nc.tensor.transpose(bank[2][:, kc * C + o * P:kc * C + (o + 1) * P],
                                              wv_sb[:, o, kc * P:(kc + 1) * P], idf[:])
            ins.then_inc(s_wvT, 1)
            pe.wait_ge(ld_ctx, 32)
            for r in range(B // 2):
                if r >= 4:
                    pe.wait_ge(s_cTlo, r - 3)
                for b in range(2):
                    for kc in range(KC):
                        ins = nc.tensor.transpose(bank[4 + r % 4][:, (b * KC + kc) * P:(b * KC + kc + 1) * P],
                                                  ctx_sb[:, 2 * r + b, kc * P:(kc + 1) * P], idf[:])
                ins.then_inc(s_cT, 1)
            pe.wait_ge(s_tern, 1)
            for kc in range(KC):
                for o in range(KC):
                    ins = nc.tensor.transpose(bank[3].bitcast(F16)[:, kc * C + o * P:kc * C + (o + 1) * P],
                                              tern[:, o, kc * P:(kc + 1) * P], idh[:])
            ins.then_inc(s_ternT, 1)
            pe.wait_ge(s_wlo, 1)
            for o in range(KC):
                ins = mm(bank[1][:, C + o * P:C + (o + 1) * P], ones[:], diag[:, o, :], start=True, stop=True)
            ins.then_inc(s_wsb, 1)
            pe.wait_ge(s_wlo, 3)
            pe.wait_ge(s_cTlo, B // 2)
            pe.wait_ge(s_clo, 1)
            pe.wait_ge(s_ternc, 2)

            def products(out, pairs, first=True, last=True):
                for j, (a, b) in enumerate(pairs):
                    ins = mm(out, a, b, start=(first and j == 0), stop=(last and j == len(pairs) - 1))
                return ins

            def transposes(k, b, banks):
                pe.wait_ge(xn_ready[k], upto(b, NT, NT))
                for kc in range(KC):
                    for i in range(NT):
                        ins = nc.tensor.transpose(bank[banks[kc]][:, i * P:(i + 1) * P],
                                                  xn[k][:, i, kc * P:(kc + 1) * P], idf[:])
                    ins.then_inc(xT_psum[k], 1)

            def query(n):
                for mc in range(KC):
                    cols = slice(mc * P, (mc + 1) * P)
                    pairs = [(bias_rows[:, 0, cols], one_rows[:])]
                    for kc in range(KC):
                        pairs += [(m_hi[:, kc, cols], xT_hi[0][:, kc, :]), (m_hi[:, kc, cols], xT_lo[0][:, kc, :]),
                                  (m_lo[:, kc, cols], xT_hi[0][:, kc, :])]
                    products(bank[2 + mc][:], pairs).then_inc(q_psum, 1)

            def value(n):
                for i in range(NT):
                    rows = slice(i * P, (i + 1) * P)
                    pairs = [(one_rows[:, 0:P], bias_rows[:, 1, :])]
                    for kc in range(KC):
                        pairs += [(xT_hi[0][:, kc, rows], wv_hi[:, kc, :]), (xT_hi[0][:, kc, rows], wv_lo[:, kc, :]),
                                  (xT_lo[0][:, kc, rows], wv_hi[:, kc, :])]
                    ins = products(bank[4 + i // 2][:, (i % 2) * C:(i % 2 + 1) * C], pairs)
                    if i % 2:
                        ins.then_inc(v_psum, 1)

            def scores(n, i):
                w = (i + 1) * P
                rows = slice(i * P, w)
                out = bank[2 + i]
                pairs = []
                for kc in range(KC):
                    pairs += [(q_hi[:, kc, rows], xT_hi[0][:, kc, 0:w]), (q_hi[:, kc, rows], xT_lo[0][:, kc, 0:w]),
                              (q_lo[:, kc, rows], xT_hi[0][:, kc, 0:w])]
                products(out[:, 0:w], pairs, last=False)
                mm(out[:, rows], idh[:], msk[:], start=False, stop=True).then_inc(scores_psum, 1)

            def prob_transposes(n, i):
                pe.wait_ge(prob_ready, upto(n, NT, i + 1))
                for j in range(i + 1):
                    ins = nc.tensor.transpose(bank[2 + i][:, j * P:(j + 1) * P], prob[:, i, j * P:(j + 1) * P],
                                              idf[:])
                ins.then_inc(pT_psum, 1)

            def attend(n, i):
                pe.wait_ge(pT_ready, upto(n, NT, i + 1))
                pairs = []
                for j in range(i + 1):
                    cols = slice(j * P, (j + 1) * P)
                    pairs += [(pT_hi[:, i, cols], v_hi[:, j, :]), (pT_hi[:, i, cols], v_lo[:, j, :]),
                              (pT_lo[:, i, cols], v_hi[:, j, :])]
                products(bank[2 + i][:, 0:C], pairs).then_inc(att_psum, 1)

            def hadamard(b):
                for i in range(NT):
                    rows = slice(i * P, (i + 1) * P)
                    pairs = []
                    for kc in range(KC):
                        pairs += [(xT_hi[2][:, kc, rows], had[:, kc, :]), (xT_lo[2][:, kc, rows], had[:, kc, :])]
                    ins = products(bank[i // 2][:, (i % 2) * C:(i % 2 + 1) * C], pairs)
                    if i % 2:
                        ins.then_inc(had_psum, 1)

            def gated_context(b):
                for i in range(NT):
                    rows = slice(i * P, (i + 1) * P)
                    ins = products(bank[6 + i // 2][:, (i % 2) * C:(i % 2 + 1) * C],
                                   [(ghl[:, rows], ctx_hi[:, b, :]), (ghl[:, rows], ctx_lo[:, b, :])])
                    if i % 2:
                        ins.then_inc(o2_psum, 1)

            def quant_transposes(b):
                for kc in range(KC):
                    for i in range(NT):
                        ins = nc.tensor.transpose(bank[0].bitcast(F16)[:, kc * T + i * P:kc * T + (i + 1) * P],
                                                  quant[:, i, kc * P:(kc + 1) * P], idh[:])
                ins.then_inc(qT_psum, 1)

            def ternary(b):
                for i in range(NT):
                    rows = slice(i * P, (i + 1) * P)
                    ins = products(bank[6 + i // 2][:, (i % 2) * C:(i % 2 + 1) * C],
                                   [(qT[:, kc, rows], ternT[:, kc, :]) for kc in range(KC)])
                    if i % 2:
                        ins.then_inc(y_psum, 1)

            def context_scores(b):
                pairs = []
                for kc in range(KC):
                    pairs += [(cT_hi[:, b, kc, :], xT_hi[1][:, kc, :]), (cT_hi[:, b, kc, :], xT_lo[1][:, kc, :]),
                              (cT_lo[:, b, kc, :], xT_hi[1][:, kc, :])]
                products(bank[6][:], pairs).then_inc(h_psum, 1)

            def body(n, parity, stages):
                if "A" in stages:
                    pe.wait_ge(xT_ready[0], upto(n, KC, KC))
                    if "B" in stages:
                        pe.wait_ge(x2_ready, upto(n - 1, NT, 2))
                    query(n)
                if "D" in stages:
                    pe.wait_ge(xT_ready[2], upto(n - 3, KC, KC))
                    hadamard(n - 3)
                if "C" in stages:
                    pe.wait_ge(g_lo_ready, upto(n - 2, 1, 1))
                    if not (isinstance(n, int) and n < 4):
                        pe.wait_ge(ytmp_ready, upto(n - 4, NT, NT))
                    gated_context(n - 2)
                if "A" in stages:
                    if "B" in stages:
                        pe.wait_ge(x2_ready, upto(n - 1, NT, NT))
                    value(n)
                    pe.wait_ge(q_ready, upto(n, KC, KC))
                    scores(n, 0)
                    scores(n, 1)
                    pe.wait_ge(v_ready, upto(n, 2, 1))
                    scores(n, 2)
                if "D" in stages:
                    pe.wait_ge(quant_ready, upto(n - 3, 1, 1))
                    quant_transposes(n - 3)
                if "A" in stages:
                    pe.wait_ge(v_ready, upto(n, 2, 2))
                    scores(n, 3)
                if "B" in stages:
                    if "C" in stages:
                        pe.wait_ge(x3_ready, upto(n - 2, NT, NT))
                    transposes(1, n - 1, (6, 7))
                if "A" in stages:
                    prob_transposes(n, 0)
                    prob_transposes(n, 1)
                if "Z" in stages:
                    if "D" in stages:
                        pe.wait_ge(qT_ready, upto(n - 3, 1, 1))
                    transposes(0, n + 1, (0, 1))
                if "D" in stages:
                    pe.wait_ge(qT_ready, upto(n - 3, 1, 1))
                    if "B" in stages:
                        pe.wait_ge(xT_ready[1], upto(n - 1, KC, KC))
                    elif "C" in stages:
                        pe.wait_ge(x3_ready, upto(n - 2, NT, NT))
                    else:
                        pe.wait_ge(ytmp_ready, upto(n - 4, NT, NT))
                    ternary(n - 3)
                if "A" in stages:
                    prob_transposes(n, 2)
                    attend(n, 0)
                    prob_transposes(n, 3)
                    attend(n, 1)
                if "B" in stages:
                    pe.wait_ge(xT_ready[1], upto(n - 1, KC, KC))
                    if "D" in stages:
                        pe.wait_ge(ytmp_ready, upto(n - 3, NT, 2))
                    context_scores(n - 1)
                if "C" in stages:
                    if "Z" in stages:
                        pe.wait_ge(xT_ready[0], upto(n + 1, KC, KC))
                    transposes(2, n - 2, (0, 1))
                if "A" in stages:
                    attend(n, 2)
                    attend(n, 3)

            steps(pe, body)


def kernel(x, ctx_1024, L0_attn_Wq, L0_attn_bq, L0_attn_Wk, L0_attn_bk, L0_attn_Wv, L0_attn_bv, L0_ffn_weight):
    import concourse.bacc as bacc
    from concourse.bass_utils import run_bass_kernel_spmd

    C = x.shape[-1]
    signs = np.array([[1.0]])
    while signs.shape[0] < C:
        signs = np.block([[signs, signs], [signs, -signs]])
    later = np.triu(np.ones((P, P)), 1) * MASKED
    consts = {
        "hada": signs.astype(np.float16),
        "ident": np.eye(P, dtype=np.float32),
        "ident16": np.eye(P, dtype=np.float16),
        "mask": later.astype(mybir.dt.np(BF16)),
    }
    data = {
        "x": x, "ctx_kv": ctx_1024, "wq": L0_attn_Wq, "bq": np.reshape(L0_attn_bq, (-1, P)).T, "wk": L0_attn_Wk, "wv": L0_attn_Wv,
        "bv": L0_attn_bv, "wffn": L0_ffn_weight,
    }
    nc = bacc.Bacc("TRN2", target_bir_lowering=False, num_devices=1)
    arrays, aps = {}, {}
    for name, a in {**data, **consts}.items():
        a = np.ascontiguousarray(a)
        arrays[f"in_{name}"] = a
        aps[name] = nc.dram_tensor(f"in_{name}", a.shape, mybir.dt.from_np(a.dtype), kind="ExternalInput").ap()
    aps["y"] = nc.dram_tensor("out_y", x.shape, F32, kind="ExternalOutput").ap()
    build(nc, **aps)
    r = run_bass_kernel_spmd(nc, [arrays], core_ids=[0])
    return r.results[0]["out_y"]
```

```python
from contextlib import ExitStack

import numpy as np

import concourse.bass as bass
from concourse import mybir

F32 = mybir.dt.float32
F16 = mybir.dt.float16
BF16 = mybir.dt.bfloat16
I32 = mybir.dt.int32
ALU = mybir.AluOpType
ACT = mybir.ActivationFunctionType
AX = mybir.AxisListType

P = 128
LN_EPS = 1e-5
X_SCALE = 2.0 ** 3
XN_UP = 2.0 * X_SCALE
W_SCALE = 2.0 ** 13
M_SCALE = 2.0 ** 3
V_SCALE = 2.0 ** -10
P_SCALE = 2.0 ** 14
G_MIN = 2.0 ** -35
ROUND = 1.5 * 2.0 ** 23
MASKED = -1e30
ACT_MAX = 7.0
QUANT_MIN = 1e-5


def upto(batch, per_batch, k):
    return batch * per_batch + k


def build(nc, x, ctx_kv, wq, bq, wk, wv, bv, wffn, hada, ident, ident16, mask, y):
    B, T, C = x.shape
    F = ctx_kv.shape[1]
    NT = T // P
    KC = C // P
    assert (NT, KC, F) == (4, 2, 64) and B % 2 == 0 and B >= 6
    SM_SCALE = float(C) ** -0.5
    Q_KEPT = M_SCALE * X_SCALE
    V_KEPT = V_SCALE * W_SCALE * X_SCALE
    S_EXP = SM_SCALE / (Q_KEPT * X_SCALE)
    H_TRUE = 1.0 / (W_SCALE * X_SCALE)
    G_KEPT = 2.0 ** -3
    H_DIM = float(C) ** 0.5
    HAD_SCALE = X_SCALE * H_DIM

    es = ExitStack()
    with es:
        def sb(name, shape, dt):
            return es.enter_context(nc.sbuf_tensor(name, shape, dt))

        def sem(name):
            return es.enter_context(nc.semaphore(name))

        banks = [es.enter_context(nc.psum_tensor(f"banks{2 * i}{2 * i + 1}", [P, 1024], F32)) for i in range(4)]
        bank = [banks[i // 2][:, (i % 2) * 512:(i % 2 + 1) * 512] for i in range(8)]

        wq_sb = sb("wq_sb", [P, KC, C], F32)
        wk_sb = sb("wk_sb", [P, KC, C], F32)
        wv_sb = sb("wv_sb", [P, KC, C], F32)
        bq_sb = sb("bq_sb", [P, KC], F32)
        bv_sb = sb("bv_sb", [64, C], F32)
        wf_sb = sb("wf_sb", [P, KC, C], F32)
        ctx_sb = sb("ctx_sb", [P, B, C], F32)
        ctx_pair = sb("ctx_pair", [P, B // 2, C], F32)
        had = sb("had", [P, P], F16)
        idf = sb("idf", [P, P], F32)
        idh = sb("idh", [P, P], F16)
        msk = sb("msk", [P, P], BF16)
        m_hi = sb("m_hi", [P, KC, C], F16)
        m_lo = sb("m_lo", [P, KC, C], F16)
        wv_hi = sb("wv_hi", [P, KC, C], F16)
        wv_lo = sb("wv_lo", [P, KC, C], F16)
        q_bias = sb("q_bias", [P, KC], F32)
        bias_rows = sb("bias_rows", [P, C], F16)
        one_rows = sb("one_rows", [P, P], F16)
        ctx_hi = sb("ctx_hi", [P, B, C], F16)
        ctx_lo = sb("ctx_lo", [P, B, C], F16)
        cT_hi = sb("cT_hi", [P, B, KC, 2, F], F16)
        cT_lo = sb("cT_lo", [P, B, KC, 2, F], F16)
        ternT = sb("ternT", [P, KC, C], F16)
        wsb = sb("wsb", [P, C], F32)
        ones = sb("ones", [P, P], F32)
        red = sb("red", [P, 4], F32)
        redw = sb("redw", [P, 4], F32)
        gmax = sb("gmax", [P, 4], F32)
        pw = sb("pw", [P, 4], F32)
        pinv = sb("pinv", [P, 4], F32)
        wsc = sb("wsc", [P, 4], F32)
        row_tmp = sb("row_tmp", [64, C], F16)
        wsum = sb("wsum", [P, KC], F32)
        wmean = sb("wmean", [P, KC], F32)
        thr = sb("thr", [P, 2, KC], F32)
        tern_p = sb("tern_p", [P, KC, C], F32)
        tern_n = sb("tern_n", [P, KC, C], F32)
        tern = sb("tern", [P, KC, C], F16)
        diag = sb("diag", [P, KC, P], F32)
        pw_sq = sb("pw_sq", [P, 1], F32)
        exp_scale = sb("exp_scale", [P, 1], F32)
        v_scale = sb("v_scale", [P, 1], F32)
        h_scale = sb("h_scale", [P, 1], F32)
        g_scale = sb("g_scale", [P, 1], F32)
        o2_scale = sb("o2_scale", [P, 1], F32)
        rnd = sb("rnd", [P, 1], F32)
        unrnd = sb("unrnd", [P, 1], F32)
        mhalf = sb("mhalf", [P, NT], F32)
        mone = sb("mone", [P, NT], F32)

        xb = [sb(f"x_{i}", [P, NT, C], F32) for i in range(2)]
        x2 = [sb(f"x2_{i}", [P, NT, C], F32) for i in range(2)]
        x3 = [sb(f"x3_{i}", [P, NT, C], F32) for i in range(2)]
        x3_last = xb[1]
        ytmp = sb("ytmp", [P, NT, C], F32)
        xn = [sb(f"xn_{i}", [P, NT, C], F32) for i in range(3)]
        sums = sb("sums", [P, NT, 2, P], F32)
        ytmp_last = xn[0]
        xT_hi = [sb(f"xT_hi_{i}", [P, KC, T], F16) for i in range(3)]
        xT_lo = [sb(f"xT_lo_{i}", [P, KC, T], F16) for i in range(3)]
        st = [sb(f"st_{i}", [P, NT, 3], F32) for i in range(3)]
        nmean = [sb(f"nmean_{i}", [P, NT], F32) for i in range(3)]
        var4 = sb("var4", [P, NT], F32)
        rstd = [sb(f"rstd_{i}", [P, NT], F32) for i in range(3)]
        q_hi = sb("q_hi", [P, KC, T], F16)
        q_lo = sb("q_lo", [P, KC, T], F16)
        v_hi = sb("v_hi", [P, NT, C], F16)
        v_lo = sb("v_lo", [P, NT, C], F16)
        negmax = sb("negmax", [P, NT], F32)
        ebias = sb("ebias", [P, NT], F32)
        prob = sb("prob", [P, NT, T], F32)
        psums = sb("psums", [P, NT], F32)
        prinv = sb("prinv", [P, NT], F32)
        oscale = sb("oscale", [P, NT], F32)
        pT_hi = sb("pT_hi", [P, NT, T], F16)
        pT_lo = sb("pT_lo", [P, NT, T], F16)
        gel = sb("gel", [P, T], F32)
        gbuf = sb("gbuf", [P, T], F32)
        ghl = sb("ghl", [P, T], F16)
        amax = sb("amax", [P, NT], F32)
        qs = [sb(f"qs_{i}", [P, NT], F32) for i in range(2)]
        qinv = sb("qinv", [P, NT], F32)
        rounded = sb("rounded", [P, NT, C], F32)
        quant = sb("quant", [P, NT, C], F16)
        qT = sb("qT", [P, KC, T], F16)

        ld_qk = sem("ld_qk")
        ld_bq = sem("ld_bq")
        ld_idf = sem("ld_idf")
        ld_v = sem("ld_v")
        ld_pair = sem("ld_pair")
        ld_ffn = sem("ld_ffn")
        ld_f16 = sem("ld_f16")
        ld_ctx = sem("ld_ctx")
        ld_x = sem("ld_x")
        st_y = sem("st_y")
        s_ones = sem("s_ones")
        m_psum = sem("m_psum")
        w_psum = sem("w_psum")
        wvT_psum = sem("wvT_psum")
        absmax_ready = sem("absmax_ready")
        allmax_ready = sem("allmax_ready")
        scales_ready = sem("scales_ready")
        w_hi_ready = sem("w_hi_ready")
        bias_ready = sem("bias_ready")
        w_ready = sem("w_ready")
        moments_ready = sem("moments_ready")
        own_vector = sem("own_vector")
        own_round = sem("own_round")
        cT_psum = sem("cT_psum")
        cT_hi_ready = sem("cT_hi_ready")
        cT_lo_ready = sem("cT_lo_ready")
        cT_ready = sem("cT_ready")
        ctx_hi_ready = sem("ctx_hi_ready")
        ctx_ready = sem("ctx_ready")
        ctx_scaled = sem("ctx_scaled")
        rowsum_ready = sem("rowsum_ready")
        tern_ready = sem("tern_ready")
        tern_psum = sem("tern_psum")
        tern_taken = sem("tern_taken")
        stats_ready = [sem(f"stats_ready_{i}") for i in range(3)]
        xn_ready = [sem(f"xn_ready_{i}") for i in range(3)]
        xT_psum = [sem(f"xT_psum_{i}") for i in range(3)]
        xT_hi_ready = [sem(f"xT_hi_ready_{i}") for i in range(3)]
        xT_ready = [sem(f"xT_ready_{i}") for i in range(3)]
        sums_ready = sem("sums_ready")
        q_psum = sem("q_psum")
        q_hi_ready = sem("q_hi_ready")
        q_ready = sem("q_ready")
        v_psum = sem("v_psum")
        v_hi_ready = sem("v_hi_ready")
        v_ready = sem("v_ready")
        scores_psum = sem("scores_psum")
        max_ready = sem("max_ready")
        ebias_ready = sem("ebias_ready")
        prob_ready = sem("prob_ready")
        pT_psum = sem("pT_psum")
        pT_hi_ready = sem("pT_hi_ready")
        pT_ready = sem("pT_ready")
        rinv_ready = sem("rinv_ready")
        oscale_ready = sem("oscale_ready")
        att_psum = sem("att_psum")
        x2_ready = sem("x2_ready")
        h_psum = sem("h_psum")
        gelu_ready = sem("gelu_ready")
        g_ready = sem("g_ready")
        g_hi_ready = sem("g_hi_ready")
        g_lo_ready = sem("g_lo_ready")
        o2_psum = sem("o2_psum")
        x3_ready = sem("x3_ready")
        had_psum = sem("had_psum")
        amax_ready = sem("amax_ready")
        qs_ready = sem("qs_ready")
        qinv_ready = sem("qinv_ready")
        round_ready = sem("round_ready")
        quant_ready = sem("quant_ready")
        qT_psum = sem("qT_psum")
        qT_ready = sem("qT_ready")
        y_psum = sem("y_psum")
        ytmp_ready = sem("ytmp_ready")
        y_ready = sem("y_ready")

        x_v = x.rearrange("b (i p) c -> b p i c", p=P)
        y_v = y.rearrange("b (i p) c -> b p i c", p=P)
        CR = 4
        CQ = 4

        def contextT(t, r):
            return t[:, CR * r:CR * (r + 1)].rearrange("p b k t f -> p (b k) t f")[:, :, 0, :]

        def steps(eng, body):
            body(0, 0, "ZAP")
            body(1, 1, "ZABQ")
            body(2, 0, "ZABCQ")
            body(3, 1, "ZABCD")
            with eng.Fori(2, B // 2 - 1) as pair:
                body(pair * 2, 0, "ZABCD")
                body(pair * 2 + 1, 1, "ZABCD")
            body(B - 2, 0, "ZABCD")
            body(B - 1, 1, "ABCD")
            body(B, 0, "BCD")
            body(B + 1, 1, "CD")
            body(B + 2, 0, "D")

        block = es.enter_context(nc.Block())

        @block.sync
        def _(sp):
            def load_x(b, parity):
                sp.dma_start(xb[parity][:], x_v[b]).then_inc(ld_x, 16)

            sp.dma_start(wq_sb[:], wq.rearrange("(k p) c -> p k c", p=P)).then_inc(ld_qk, 16)
            sp.dma_start(wk_sb[:], wk.rearrange("(k p) c -> p k c", p=P)).then_inc(ld_qk, 16)
            load_x(0, 0)
            sp.dma_start(idf[:], ident).then_inc(ld_idf, 16)
            sp.dma_start(wv_sb[:], wv.rearrange("(k p) c -> p k c", p=P)).then_inc(ld_v, 16)
            sp.dma_start(ctx_pair[:], ctx_kv.rearrange("(r h) f c -> (h f) r c", h=2)).then_inc(ld_pair, 16)
            sp.wait_ge(ld_x, 16)
            load_x(1, 1)
            sp.dma_start(wf_sb[:], wffn.rearrange("(k p) c -> p k c", p=P)).then_inc(ld_ffn, 16)
            for h in range(2):
                sp.dma_start(ctx_sb[h * F:(h + 1) * F], ctx_kv.rearrange("b f c -> f b c")).then_inc(ld_ctx, 16)

            def body(n, parity, stages):
                if stages == "D":
                    for j in range(2):
                        tiles = slice(2 * j, 2 * j + 2)
                        sp.wait_ge(y_ready, upto(n - 3, 1, 1) + j)
                        sp.dma_start(y_v[n - 3][:, tiles], x3_last[:, tiles]).then_inc(st_y, 16)
                elif "D" in stages:
                    sp.wait_ge(y_ready, upto(n - 3, 1, 1))
                    sp.dma_start(y_v[n - 3], x3[1 - parity][:]).then_inc(st_y, 16)
                if "A" in stages and "Z" in stages:
                    if isinstance(n, int) and n + 2 >= B:
                        return
                    sp.wait_ge(x2_ready, upto(n, NT, NT))
                    load_x(n + 2, parity)

            steps(sp, body)
            sp.wait_ge(st_y, 16 * (B + 1))

        @block.gpsimd
        def _(pool):
            nc.gpsimd.memset(ones[:], 1.0)
            nc.gpsimd.memset(rnd[:], ROUND)
            nc.gpsimd.memset(unrnd[:], -ROUND)
            nc.gpsimd.memset(mhalf[:], -0.5)
            nc.gpsimd.memset(mone[:], -1.0)
            nc.gpsimd.memset(bias_rows[:], 0.0)
            nc.gpsimd.memset(one_rows[:], 0.0).then_inc(s_ones, 1)
            pool.wait_ge(s_ones, 1)
            nc.gpsimd.memset(one_rows[0:1, :], X_SCALE)
            nc.gpsimd.memset(one_rows[32:33, :], X_SCALE).then_inc(s_ones, 1)
            pool.wait_ge(s_ones, 2)

            def largest(cols, k):
                pool.wait_ge(absmax_ready, k)
                nc.gpsimd.partition_all_reduce(gmax[:, cols], red[:, cols], P, bass.bass_isa.ReduceOp.max)\
                    .then_inc(allmax_ready, 1)

            def halves(b, ops=(ALU.add, ALU.subtract)):
                pool.wait_ge(xn_ready[2], upto(b, NT, NT))
                for j, op in enumerate(ops):
                    nc.gpsimd.tensor_tensor(sums[:, :, j, :], xn[2][:, :, 0:P], xn[2][:, :, P:2 * P], op)\
                        .then_inc(sums_ready, 1)

            def gated_lo(b):
                pool.drain()
                pool.wait_ge(g_hi_ready, upto(b, 1, 1))
                nc.gpsimd.tensor_tensor(ghl[F:2 * F, :], gbuf[F:2 * F, :], ghl[F:2 * F, :], ALU.subtract)\
                    .then_inc(g_lo_ready, 1)
                pool.drain()

            def ternary_weights():
                pool.wait_ge(rowsum_ready, 1)
                nc.gpsimd.tensor_scalar(wmean[:], wsum[:], 1.0 / C, QUANT_MIN, ALU.mult, ALU.max)
                pool.drain()
                nc.gpsimd.tensor_scalar(thr[:, 0, :], wmean[:], 0.5, None, ALU.mult)
                nc.gpsimd.tensor_scalar(thr[:, 1, :], wmean[:], -0.5, None, ALU.mult)
                pool.drain()
                for k in range(KC):
                    nc.gpsimd.tensor_scalar(diag[:, k, :], idf[:], wmean[:, k:k + 1], None, ALU.mult)
                    nc.gpsimd.tensor_scalar(tern_p[:, k, :], wf_sb[:, k, :], thr[:, 0, k:k + 1], None, ALU.is_gt)
                    nc.gpsimd.tensor_scalar(tern_n[:, k, :], wf_sb[:, k, :], thr[:, 1, k:k + 1], None, ALU.is_lt)
                pool.drain()
                nc.gpsimd.tensor_tensor(tern[:], tern_p[:], tern_n[:], ALU.subtract).then_inc(tern_ready, 1)

            def context_lo(parts):
                for q in parts:
                    part = slice(q * CQ, (q + 1) * CQ)
                    pool.wait_ge(ctx_hi_ready, q + 1)
                    nc.gpsimd.tensor_tensor(ctx_lo[:, part], ctx_sb[:, part], ctx_hi[:, part], ALU.subtract)\
                        .then_inc(ctx_ready, 1)

            def moments(k, b):
                pool.wait_ge(stats_ready[k], upto(b, 1, 1))
                nc.gpsimd.tensor_tensor(nmean[k][:], st[k][:, :, 1], mone[:], ALU.mult)
                nc.gpsimd.tensor_scalar(var4[:], st[k][:, :, 2], 4.0 / C, 4.0 * LN_EPS, ALU.mult, ALU.add)
                pool.drain()
                return nc.gpsimd.tensor_tensor(rstd[k][:], var4[:], mhalf[:], ALU.pow)

            def normalise(k, b, src, tiles=range(NT)):
                ins = moments(k, b)
                if len(tiles) < NT:
                    ins.then_inc(moments_ready, 1)
                pool.drain()
                for i in tiles:
                    nc.gpsimd.tensor_scalar(xn[k][:, i, :], src[:, i, :], nmean[k][:, i:i + 1], rstd[k][:, i:i + 1],
                                            ALU.add, ALU.mult).then_inc(xn_ready[k], 1)

            def body(n, parity, stages):
                if "B" in stages:
                    normalise(1, n - 1, x2[1 - parity], range(NT) if "A" in stages else (2, 3))
                if "Z" in stages:
                    normalise(0, n + 1, xb[1 - parity])
                if "P" in stages:
                    ternary_weights()
                    context_lo((0, 1))
                if "C" in stages:
                    if "A" in stages:
                        normalise(2, n - 2, x3[parity])
                        halves(n - 2)
                    elif "B" in stages:
                        normalise(2, n - 2, x3[parity])
                        halves(n - 2, (ALU.add,))
                    else:
                        normalise(2, n - 2, x3_last, (2, 3))
                        halves(n - 2, (ALU.add,))
                if stages == "CD":
                    for b, buf in ((n - 4, x3[parity]), (n - 3, x3[1 - parity])):
                        pool.wait_ge(ytmp_ready, upto(b, NT, NT))
                        nc.gpsimd.tensor_tensor(buf[:], buf[:], ytmp[:], ALU.add).then_inc(y_ready, 1)
                elif stages == "D":
                    for i in range(NT):
                        pool.wait_ge(ytmp_ready, upto(n - 3, NT, i + 1))
                        ins = nc.gpsimd.tensor_tensor(x3_last[:, i, :], x3_last[:, i, :], ytmp_last[:, i, :],
                                                      ALU.add)
                        if i % 2:
                            ins.then_inc(y_ready, 1)
                elif "D" in stages and "A" in stages:
                    pool.wait_ge(ytmp_ready, upto(n - 3, NT, NT))
                    nc.gpsimd.tensor_tensor(x3[1 - parity][:], x3[1 - parity][:], ytmp[:], ALU.add)\
                        .then_inc(y_ready, 1)
                if "B" in stages and "A" in stages:
                    gated_lo(n - 1)
                if "Q" in stages:
                    context_lo((n + 1,))

            moments(0, 0).then_inc(moments_ready, 1)
            largest(slice(0, 2), 1)
            pool.wait_ge(xn_ready[0], NT)
            largest(slice(2, 3), 2)
            steps(pool, body)

        @block.scalar
        def _(act):
            act.dma_start(bq_sb[:], bq).then_inc(ld_bq, 16)
            for r in (0, 32):
                act.dma_start(bv_sb[r:r + 1, :], bv.rearrange("(a c) -> a c", a=1)).then_inc(ld_v, 16)
            act.dma_start(idh[:], ident16).then_inc(ld_f16, 16)
            act.dma_start(msk[:], mask).then_inc(ld_f16, 16)
            act.dma_start(had[:], hada).then_inc(ld_f16, 16)

            def hi_transposed(k, b, banks):
                for kc in range(KC):
                    act.wait_ge(xT_psum[k], upto(b, KC, kc + 1))
                    nc.scalar.activation(xT_hi[k][:, kc, :], bank[banks[kc]][:], ACT.Copy, scale=XN_UP)\
                        .then_inc(xT_hi_ready[k], 1)

            def exps(b, tiles):
                for i in tiles:
                    w = (i + 1) * P
                    act.wait_ge(ebias_ready, upto(b, 2, i // 2 + 1))
                    nc.scalar.activation(prob[:, i, 0:w], bank[2 + i][:, 0:w], ACT.Exp,
                                         bias=ebias[:, i:i + 1], scale=exp_scale[:, 0:1],
                                         accum_out=psums[:, i:i + 1]).then_inc(prob_ready, 1)

            def prob_hi(b, tiles):
                for i in tiles:
                    w = (i + 1) * P
                    act.wait_ge(pT_psum, upto(b, NT, i + 1))
                    nc.scalar.activation(pT_hi[:, i, 0:w], bank[2 + i][:, 0:w], ACT.Copy,
                                         scale=P_SCALE).then_inc(pT_hi_ready, 1)

            def query_hi(b):
                for kc in range(KC):
                    act.wait_ge(q_psum, upto(b, KC, kc + 1))
                    nc.scalar.activation(q_hi[:, kc, :], bank[2 + kc][:], ACT.Identity,
                                         bias=q_bias[:, kc:kc + 1])\
                        .then_inc(q_hi_ready, 1)

            def value_hi(b, j):
                act.wait_ge(v_psum, upto(b, 2, j + 1))
                nc.scalar.activation(v_hi[:, 2 * j:2 * j + 2, :], bank[4 + j][:].rearrange("p (i c) -> p i c", i=2),
                                     ACT.Copy, scale=V_SCALE).then_inc(v_hi_ready, 1)

            def context_hi(parts):
                for q in parts:
                    part = slice(q * CQ, (q + 1) * CQ)
                    nc.scalar.activation(ctx_sb[:, part], ctx_sb[:, part], ACT.Copy, scale=wsc[:, 2:3])\
                        .then_inc(ctx_scaled, 1)
                for q in parts:
                    part = slice(q * CQ, (q + 1) * CQ)
                    act.wait_ge(ctx_scaled, q + 1)
                    nc.scalar.activation(ctx_hi[:, part], ctx_sb[:, part], ACT.Copy).then_inc(ctx_hi_ready, 1)

            def contextT_hi(rounds):
                for r in rounds:
                    act.wait_ge(cT_psum, r + 1)
                    nc.scalar.activation(contextT(cT_hi, r),
                                         bank[6 + r % 2][:].rearrange("p (bk f) -> p bk f", f=F),
                                         ACT.Copy, scale=wsc[:, 2:3]).then_inc(cT_hi_ready, 1)

            act.wait_ge(scales_ready, 1)
            nc.scalar.activation(m_hi[:], bank[4][:].rearrange("p (k c) -> p k c", k=KC), ACT.Copy,
                                 scale=wsc[:, 0:1]).then_inc(w_hi_ready, 1)
            hi_transposed(0, 0, (0, 1))
            act.wait_ge(wvT_psum, 1)
            nc.scalar.activation(wv_hi[:], bank[7][:].rearrange("p (k c) -> p k c", k=KC), ACT.Copy,
                                 scale=wsc[:, 1:2]).then_inc(w_hi_ready, 1)
            act.wait_ge(s_ones, 2)

            def rounding(b, tiles=range(NT), bank_of=lambda i: bank[i // 2]):
                act.wait_ge(qinv_ready, upto(b, 1, 1))
                for i in tiles:
                    nc.scalar.activation(rounded[:, i, :], bank_of(i)[:, (i % 2) * C:(i % 2 + 1) * C],
                                         ACT.Identity, bias=rnd[:, 0:1], scale=qinv[:, i:i + 1])\
                        .then_inc(round_ready, 1)

            def quantised(b, tiles=range(NT)):
                if len(tiles) < NT:
                    act.wait_ge(qT_psum, upto(b - 1, 1, 1))
                act.wait_ge(round_ready, upto(b, NT, len(tiles)))
                nc.scalar.activation(quant[:, 0:len(tiles)], rounded[:, 0:len(tiles)], ACT.Identity,
                                     bias=unrnd[:, 0:1]).then_inc(quant_ready, 1)

            def quant_transposed(b):
                act.wait_ge(qT_psum, upto(b, 1, 1))
                nc.scalar.activation(qT[:], bank[0].bitcast(F16)[:, :].rearrange("p (k t) -> p k t", k=KC),
                                     ACT.Copy).then_inc(qT_ready, 1)

            def gelu(b):
                act.wait_ge(h_psum, upto(b, 1, 1))
                nc.scalar.activation(gel[:], bank[6][:], ACT.Gelu, scale=h_scale[:, 0:1]).then_inc(gelu_ready, 1)

            def gated_hi(b):
                act.wait_ge(g_ready, upto(b, 1, 1))
                nc.scalar.activation(ghl[:], gbuf[:], ACT.Copy).then_inc(g_hi_ready, 1)

            def last_steps(n, stages):
                if stages == "BCD":
                    rounding(n - 3)
                    hi_transposed(1, n - 1, (6, 7))
                    quantised(n - 3)
                    quant_transposed(n - 3)
                    gelu(n - 1)
                    gated_hi(n - 1)
                    hi_transposed(2, n - 2, (0, 1))
                elif stages == "CD":
                    rounding(n - 3)
                    quantised(n - 3)
                    hi_transposed(2, n - 2, (6, 7))
                    quant_transposed(n - 3)
                else:
                    rounding(n - 3, (0, 1), lambda i: bank[2])
                    quantised(n - 3, (0, 1))
                    quant_transposed(n - 3)

            def body(n, parity, stages):
                if "A" not in stages:
                    last_steps(n, stages)
                    return
                if "A" in stages:
                    query_hi(n)
                    if "P" in stages:
                        act.wait_ge(scales_ready, 2)
                        contextT_hi((0, 1))
                    value_hi(n, 0)
                if "D" in stages:
                    rounding(n - 3)
                if "A" in stages:
                    value_hi(n, 1)
                if "D" in stages:
                    quantised(n - 3)
                if "A" in stages:
                    exps(n, (0, 1))
                    if "P" in stages:
                        contextT_hi((2, 3))
                if "D" in stages:
                    quant_transposed(n - 3)
                if "A" in stages:
                    prob_hi(n, (0,))
                if "B" in stages:
                    hi_transposed(1, n - 1, (6, 7))
                if "A" in stages:
                    exps(n, (2, 3))
                    prob_hi(n, (1,))
                    prob_hi(n, (2,))
                    prob_hi(n, (3,))
                if "Z" in stages:
                    hi_transposed(0, n + 1, (0, 1))
                if "P" in stages:
                    act.wait_ge(ld_ctx, 32)
                    context_hi((0, 1))
                    act.wait_ge(tern_psum, 1)
                    nc.scalar.activation(ternT[:], bank[1].bitcast(F16)[:, 0:512].rearrange("p (k c) -> p k c", k=KC),
                                         ACT.Copy).then_inc(tern_taken, 1)
                    nc.scalar.activation(wsb[:], bank[1][:, 256:512], ACT.Copy, scale=1.0 / HAD_SCALE)\
                        .then_inc(tern_taken, 1)
                if "B" in stages:
                    gelu(n - 1)
                if "C" in stages:
                    hi_transposed(2, n - 2, (0, 1))
                if "B" in stages:
                    gated_hi(n - 1)
                if "Q" in stages:
                    context_hi((n + 1,))
            steps(act, body)

        @block.vector
        def _(dve):
            done = [0]

            def link(ins):
                done[0] += 1
                ins.then_inc(own_vector, 1)
                dve.wait_ge(own_vector, done[0])

            def stats(k, b, src):
                for j in range(2):
                    tiles = slice(2 * j, 2 * j + 2)
                    ins = nc.vector.bn_stats(st[k][:, tiles, :].rearrange("p i s -> p (i s)"),
                                             src[:, tiles, :].rearrange("p i c -> p c i"))
                ins.then_inc(stats_ready[k], 1)

            def powers(cols):
                link(nc.vector.tensor_scalar(gmax[:, cols], gmax[:, cols], G_MIN, None, ALU.max))
                link(nc.vector.tensor_scalar(pw[:, cols].bitcast(I32), gmax[:, cols].bitcast(I32), 0x7F800000, None,
                                             ALU.bitwise_and))
                link(nc.vector.reciprocal(pinv[:, cols], pw[:, cols]))

            def prepare_weights():
                dve.wait_ge(s_ones, 2)
                dve.wait_ge(ld_x, 16)
                stats(0, 0, xb[0])
                dve.wait_ge(ld_v, 48)
                nc.vector.tensor_reduce(red[:, 1:2], wv_sb[:], AX.XY, ALU.max, apply_absolute_value=True)
                nc.vector.tensor_reduce(redw[0:1, 1:2], bv_sb[0:1, :], AX.X, ALU.max, apply_absolute_value=True)
                dve.wait_ge(m_psum, 1)
                nc.vector.tensor_reduce(red[:, 0:1], bank[4][:], AX.X, ALU.max, apply_absolute_value=True)
                dve.wait_ge(w_psum, 1)
                link(nc.vector.tensor_reduce(redw[:, 0:1], bank[5][:, 0:KC], AX.X, ALU.max, apply_absolute_value=True))
                nc.vector.tensor_tensor(red[0:1, 1:2], red[0:1, 1:2], redw[0:1, 1:2], ALU.max)
                nc.vector.tensor_tensor(red[:, 0:1], red[:, 0:1], redw[:, 0:1], ALU.max).then_inc(absmax_ready, 1)
                dve.wait_ge(moments_ready, 1)
                for i in range(NT):
                    nc.vector.tensor_scalar(xn[0][:, i, :], xb[0][:, i, :], nmean[0][:, i:i + 1], rstd[0][:, i:i + 1],
                                            ALU.add, ALU.mult).then_inc(xn_ready[0], 1)
                dve.wait_ge(allmax_ready, 1)
                powers(slice(0, 2))
                nc.vector.tensor_scalar(wsc[:, 0:1], pinv[:, 0:1], M_SCALE, None, ALU.mult)
                nc.vector.tensor_scalar(wsc[:, 1:2], pinv[:, 1:2], W_SCALE, None, ALU.mult).then_inc(scales_ready, 1)
                nc.vector.tensor_scalar(exp_scale[:], pw[:, 0:1], S_EXP, None, ALU.mult)
                nc.vector.tensor_scalar(v_scale[:], pw[:, 1:2], 1.0 / (P_SCALE * V_KEPT), None, ALU.mult)
                dve.wait_ge(scales_ready, 1)
                nc.vector.tensor_scalar(q_bias[:], bank[5][:, 0:KC], wsc[:, 0:1], X_SCALE, ALU.mult, ALU.mult)\
                    .then_inc(bias_ready, 1)
                weight_lo(0, bank[4], m_lo, m_hi)

            def weight_lo(k, src, lo, hi):
                dve.wait_ge(w_hi_ready, k + 1)
                nc.vector.scalar_tensor_tensor(lo[:], src[:].rearrange("p (k c) -> p k c", k=KC),
                                               wsc[:, k:k + 1], hi[:], ALU.mult, ALU.subtract).then_inc(w_ready, 1)

            def prepare_value_weights():
                for r in (0, 32):
                    ins = nc.vector.tensor_scalar(row_tmp[r:r + 1, :], bv_sb[r:r + 1, :], wsc[r:r + 1, 1:2], None,
                                                  ALU.mult)
                link(ins)
                nc.vector.tensor_copy(bias_rows[0:1, :], row_tmp[0:1, :])
                nc.vector.scalar_tensor_tensor(bias_rows[32:33, :], bv_sb[32:33, :], wsc[32:33, 1:2],
                                               row_tmp[32:33, :], ALU.mult, ALU.subtract).then_inc(bias_ready, 1)
                weight_lo(1, bank[7], wv_lo, wv_hi)

            def context_max():
                dve.wait_ge(ld_pair, 16)
                nc.vector.tensor_reduce(red[:, 2:3], ctx_pair[:], AX.XY, ALU.max, apply_absolute_value=True)\
                    .then_inc(absmax_ready, 1)

            def context_scale():
                dve.wait_ge(allmax_ready, 2)
                powers(slice(2, 3))
                nc.vector.tensor_scalar(wsc[:, 2:3], pinv[:, 2:3], W_SCALE, None, ALU.mult).then_inc(scales_ready, 1)
                nc.vector.tensor_scalar(h_scale[:], pw[:, 2:3], H_TRUE, None, ALU.mult)
                nc.vector.tensor_scalar(g_scale[:], pinv[:, 2:3], G_KEPT * H_TRUE, None, ALU.mult)
                link(nc.vector.tensor_scalar(pw_sq[:], pw[:, 2:3], pw[:, 2:3], None, ALU.mult))
                nc.vector.tensor_scalar(o2_scale[:], pw_sq[:], pw[:, 2:3], 1.0 / (G_KEPT * W_SCALE),
                                        ALU.mult, ALU.mult)

            def contextT_lo(rounds):
                for r in rounds:
                    dve.wait_ge(cT_hi_ready, r + 1)
                    nc.vector.scalar_tensor_tensor(contextT(cT_lo, r),
                                                   bank[6 + r % 2][:].rearrange("p (bk f) -> p bk f", f=F),
                                                   wsc[:, 2:3], contextT(cT_hi, r),
                                                   ALU.mult, ALU.subtract).then_inc(cT_lo_ready, 1)

            def contextT_twice():
                dve.wait_ge(cT_lo_ready, B // CR)
                for t in (cT_hi, cT_lo):
                    v = t[:].rearrange("p b k t f -> p (b k) t f")
                    nc.vector.tensor_copy(v[:, :, 1, :], v[:, :, 0, :]).then_inc(cT_ready, 1)

            def lo_transposed(k, b, at):
                for kc in range(KC):
                    dve.wait_ge(xT_hi_ready[k], upto(b, KC, kc + 1))
                    nc.vector.scalar_tensor_tensor(xT_lo[k][:, kc, :], bank[at[kc]][:], XN_UP, xT_hi[k][:, kc, :],
                                                   ALU.mult, ALU.subtract).then_inc(xT_ready[k], 1)

            def maximum(b, i):
                dve.wait_ge(scores_psum, upto(b, NT, i + 1))
                nc.vector.tensor_reduce(negmax[:, i:i + 1], bank[2 + i][:, 0:(i + 1) * P], AX.X, ALU.max,
                                        negate=True).then_inc(max_ready, 1)

            def exp_bias(b, pair):
                dve.wait_ge(max_ready, upto(b, NT, 2 * pair + 2))
                nc.vector.tensor_scalar(ebias[:, 2 * pair:2 * pair + 2], negmax[:, 2 * pair:2 * pair + 2],
                                        exp_scale[:, 0:1], None, ALU.mult).then_inc(ebias_ready, 1)

            def prob_lo(b, tiles):
                for i in tiles:
                    w = (i + 1) * P
                    dve.wait_ge(pT_hi_ready, upto(b, NT, i + 1))
                    nc.vector.scalar_tensor_tensor(pT_lo[:, i, 0:w], bank[2 + i][:, 0:w], P_SCALE,
                                                   pT_hi[:, i, 0:w], ALU.mult, ALU.subtract).then_inc(pT_ready, 1)

            def attended(b, parity, tiles):
                for i in tiles:
                    dve.wait_ge(att_psum, upto(b, NT, i + 1))
                    nc.vector.scalar_tensor_tensor(x2[parity][:, i, :], bank[2 + i][:, 0:C], oscale[:, i:i + 1],
                                                   xb[parity][:, i, :], ALU.mult, ALU.add).then_inc(x2_ready, 1)

            def query_lo(b):
                for kc in range(KC):
                    dve.wait_ge(q_hi_ready, upto(b, KC, kc + 1))
                    nc.vector.scalar_tensor_tensor(q_lo[:, kc, :], bank[2 + kc][:], q_bias[:, kc:kc + 1],
                                                   q_hi[:, kc, :], ALU.add, ALU.subtract).then_inc(q_ready, 1)

            def value_lo(b, j):
                dve.wait_ge(v_hi_ready, upto(b, 2, j + 1))
                nc.vector.scalar_tensor_tensor(
                    v_lo[:, 2 * j:2 * j + 2, :], bank[4 + j][:].rearrange("p (i c) -> p i c", i=2), V_SCALE,
                    v_hi[:, 2 * j:2 * j + 2, :], ALU.mult, ALU.subtract).then_inc(v_ready, 1)

            def row_maxima(b, at=(0, 1)):
                dve.wait_ge(had_psum, upto(b, 2, 2))
                nc.vector.tensor_reduce(amax[:], banks[at[0] // 2][:].rearrange("p (i c) -> p i c", i=NT), AX.X,
                                        ALU.max, apply_absolute_value=True).then_inc(amax_ready, 1)

            def quant_scale(b, parity):
                dve.wait_ge(amax_ready, upto(b, 1, 1))
                nc.vector.tensor_scalar(qs[parity][:], amax[:], QUANT_MIN * HAD_SCALE, 1.0 / ACT_MAX, ALU.max, ALU.mult)\
                    .then_inc(qs_ready, 1)

            def quant_inverse(b, parity):
                dve.wait_ge(qs_ready, upto(b, 1, 1))
                nc.vector.reciprocal(qinv[:], qs[parity][:]).then_inc(qinv_ready, 1)

            def cross_attended(b, out, parity, banks):
                for j in range(2):
                    tiles = slice(2 * j, 2 * j + 2)
                    dve.wait_ge(o2_psum, upto(b, 2, j + 1))
                    nc.vector.scalar_tensor_tensor(out[:, tiles, :].rearrange("p i c -> p (i c)"),
                                                   bank[banks[j]][:], o2_scale[:, 0:1],
                                                   x2[parity][:, tiles, :].rearrange("p i c -> p (i c)"),
                                                   ALU.mult, ALU.add).then_inc(x3_ready, 1)

            def cross_gated(b):
                dve.wait_ge(gelu_ready, upto(b, 1, 1))
                nc.vector.scalar_tensor_tensor(gbuf[:], bank[6][:], g_scale[:, 0:1], gel[:], ALU.mult,
                                               ALU.mult).then_inc(g_ready, 1)

            def cross_gated_lo(b):
                dve.wait_ge(g_hi_ready, upto(b, 1, 1))
                nc.vector.tensor_tensor(ghl[F:2 * F, :], gbuf[F:2 * F, :], ghl[F:2 * F, :], ALU.subtract)\
                    .then_inc(g_lo_ready, 1)

            def normalised(k, src):
                for i in (0, 1):
                    nc.vector.tensor_scalar(xn[k][:, i, :], src[:, i, :], nmean[k][:, i:i + 1], rstd[k][:, i:i + 1],
                                            ALU.add, ALU.mult).then_inc(xn_ready[k], 1)

            def ffn_scaled(b, parity, j, banks, out=ytmp):
                dve.wait_ge(y_psum, upto(b, 2, j + 1))
                for i in (2 * j, 2 * j + 1):
                    nc.vector.scalar_tensor_tensor(out[:, i, :], bank[banks[j]][:, (i % 2) * C:(i % 2 + 1) * C],
                                                   qs[parity][:, i:i + 1], wsb[:], ALU.mult, ALU.mult)\
                        .then_inc(ytmp_ready, 1)

            prepare_weights()
            lo_transposed(0, 0, (0, 1))
            prepare_value_weights()
            context_max()
            dve.wait_ge(ld_ffn, 16)
            nc.vector.tensor_reduce(wsum[:], wf_sb[:], AX.X, ALU.add, apply_absolute_value=True)\
                .then_inc(rowsum_ready, 1)

            def differences(b):
                dve.wait_ge(xn_ready[2], upto(b, NT, NT))
                dve.wait_ge(xT_psum[2], upto(b - 1, KC, KC))
                nc.vector.tensor_tensor(sums[:, :, 1, :], xn[2][:, :, 0:P], xn[2][:, :, P:2 * P], ALU.subtract)\
                    .then_inc(sums_ready, 1)

            def last_steps(n, parity, stages):
                if stages == "BCD":
                    row_maxima(n - 3)
                    quant_scale(n - 3, 1 - parity)
                    quant_inverse(n - 3, 1 - parity)
                    dve.wait_ge(moments_ready, 2)
                    normalised(1, x2[1 - parity])
                    dve.wait_ge(st_y, upto(n - 4, 16, 16))
                    cross_attended(n - 2, x3[parity], parity, (2, 3))
                    dve.wait_ge(x3_ready, upto(n - 2, 2, 2))
                    stats(2, n - 2, x3[parity])
                    lo_transposed(1, n - 1, (6, 7))
                    differences(n - 2)
                    cross_gated(n - 1)
                    cross_gated_lo(n - 1)
                    lo_transposed(2, n - 2, (0, 1))
                    cross_attended(n - 1, x3_last, 1 - parity, (2, 3))
                    dve.wait_ge(x3_ready, upto(n - 1, 2, 2))
                    stats(2, n - 1, x3_last)
                elif stages == "CD":
                    row_maxima(n - 3)
                    quant_scale(n - 3, 1 - parity)
                    quant_inverse(n - 3, 1 - parity)
                    dve.wait_ge(moments_ready, 3)
                    normalised(2, x3_last)
                    differences(n - 2)
                    dve.wait_ge(y_ready, upto(n - 5, 1, 1))
                    ffn_scaled(n - 4, parity, 0, (4, 5))
                    ffn_scaled(n - 4, parity, 1, (4, 5))
                    lo_transposed(2, n - 2, (6, 7))
                else:
                    row_maxima(n - 3, (2, 3))
                    quant_scale(n - 3, 1 - parity)
                    dve.wait_ge(quant_ready, upto(n - 4, 1, 1))
                    quant_inverse(n - 3, 1 - parity)
                    dve.wait_ge(qinv_ready, upto(n - 3, 1, 1))
                    for i in (2, 3):
                        nc.vector.tensor_scalar(rounded[:, i, :], bank[3][:, (i % 2) * C:(i % 2 + 1) * C],
                                                qinv[:, i:i + 1], ROUND, ALU.mult, ALU.add)\
                            .then_inc(own_round, 1)
                    dve.wait_ge(own_round, 2)
                    dve.wait_ge(qT_psum, upto(n - 4, 1, 1))
                    nc.vector.tensor_scalar(quant[:, 2:4], rounded[:, 2:4], -ROUND, None, ALU.add)\
                        .then_inc(quant_ready, 1)
                    dve.wait_ge(y_ready, upto(n - 5, 1, 1))
                    ffn_scaled(n - 4, parity, 0, (4, 5))
                    ffn_scaled(n - 4, parity, 1, (4, 5))
                    ffn_scaled(n - 3, 1 - parity, 0, (6, 7), ytmp_last)
                    ffn_scaled(n - 3, 1 - parity, 1, (6, 7), ytmp_last)

            def body(n, parity, stages):
                known = isinstance(n, int)
                if "A" not in stages:
                    last_steps(n, parity, stages)
                    return
                if "P" in stages:
                    context_scale()
                if "A" in stages:
                    query_lo(n)
                if "D" in stages:
                    row_maxima(n - 3)
                    quant_scale(n - 3, 1 - parity)
                    quant_inverse(n - 3, 1 - parity)
                if "A" in stages:
                    value_lo(n, 0)
                if "Z" in stages:
                    dve.wait_ge(ld_x, upto(n + 1, 16, 16))
                    stats(0, n + 1, xb[1 - parity])
                if "C" in stages:
                    if not (known and n < 4):
                        dve.wait_ge(st_y, upto(n - 4, 16, 16))
                    cross_attended(n - 2, x3[parity], parity, (6, 7))
                if "A" in stages:
                    value_lo(n, 1)
                    if "P" in stages:
                        contextT_lo((0, 1))
                    maximum(n, 0)
                    maximum(n, 1)
                    exp_bias(n, 0)
                    maximum(n, 2)
                if "C" in stages:
                    dve.wait_ge(x3_ready, upto(n - 2, 2, 2))
                    stats(2, n - 2, x3[parity])
                if "A" in stages:
                    maximum(n, 3)
                    exp_bias(n, 1)
                    prob_lo(n, (0,))
                if "B" in stages:
                    lo_transposed(1, n - 1, (6, 7))
                if "D" in stages:
                    if not (known and n < 4):
                        dve.wait_ge(y_ready, upto(n - 4, 1, 1))
                    ffn_scaled(n - 3, 1 - parity, 0, (6, 7))
                    ffn_scaled(n - 3, 1 - parity, 1, (6, 7))
                if "A" in stages:
                    dve.wait_ge(prob_ready, upto(n, NT, NT))
                    nc.vector.reciprocal(prinv[:], psums[:]).then_inc(rinv_ready, 1)
                    prob_lo(n, (1,))
                    dve.wait_ge(rinv_ready, upto(n, 1, 1))
                    nc.vector.tensor_scalar(oscale[:], prinv[:], v_scale[:, 0:1], None, ALU.mult)\
                        .then_inc(oscale_ready, 1)
                    if "P" in stages:
                        contextT_lo((2, 3))
                    prob_lo(n, (2,))
                    prob_lo(n, (3,))
                    dve.wait_ge(oscale_ready, upto(n, 1, 1))
                    attended(n, parity, (0,))
                if "Z" in stages:
                    lo_transposed(0, n + 1, (0, 1))
                if "A" in stages:
                    attended(n, parity, (1,))
                if "B" in stages:
                    cross_gated(n - 1)
                if "A" in stages:
                    attended(n, parity, (2,))
                    attended(n, parity, (3,))
                if "C" in stages:
                    lo_transposed(2, n - 2, (0, 1))
                if "A" in stages:
                    dve.wait_ge(x2_ready, upto(n, NT, NT))
                    stats(1, n, x2[parity])
                if "P" in stages:
                    contextT_twice()
            steps(dve, body)

        @block.tensor
        def _(pe):
            mm = nc.tensor.matmul
            pe.wait_ge(ld_qk, 32)
            for kc in range(KC):
                for o in range(KC):
                    ins = mm(bank[4][:, kc * C:(kc + 1) * C], wq_sb[:, o, kc * P:(kc + 1) * P], wk_sb[:, o, :],
                             start=(o == 0), stop=(o == KC - 1))
            ins.then_inc(m_psum, 1)
            pe.wait_ge(ld_bq, 16)
            for kc in range(KC):
                for o in range(KC):
                    ins = mm(bank[5][:, kc:kc + 1], wk_sb[:, o, kc * P:(kc + 1) * P], bq_sb[:, o:o + 1],
                             start=(o == 0), stop=(o == KC - 1))
            ins.then_inc(w_psum, 1)
            pe.wait_ge(ld_idf, 16)
            pe.wait_ge(ld_v, 48)
            for kc in range(KC):
                for o in range(KC):
                    ins = nc.tensor.transpose(bank[7][:, kc * C + o * P:kc * C + (o + 1) * P],
                                              wv_sb[:, o, kc * P:(kc + 1) * P], idf[:])
            ins.then_inc(wvT_psum, 1)

            def context_transposes(rounds):
                for r in rounds:
                    if r == 1:
                        pe.wait_ge(w_ready, 2)
                    elif r > 1:
                        pe.wait_ge(cT_lo_ready, r - 1)
                    for kc in range(KC):
                        for j in range(CR // 2):
                            ins = nc.tensor.transpose(
                                bank[6 + r % 2][:].rearrange("p (j h k f) -> p j h k f", h=2, k=KC, f=F)[:, j, :, kc, :],
                                ctx_pair[:, CR // 2 * r + j, kc * P:(kc + 1) * P], idf[:])
                    ins.then_inc(cT_psum, 1)

            def ternary_transposes():
                pe.wait_ge(tern_ready, 1)
                pe.wait_ge(ld_f16, 48)
                for kc in range(KC):
                    for o in range(KC):
                        nc.tensor.transpose(bank[1].bitcast(F16)[:, kc * C + o * P:kc * C + (o + 1) * P],
                                            tern[:, o, kc * P:(kc + 1) * P], idh[:])
                for o in range(KC):
                    ins = mm(bank[1][:, C + o * P:C + (o + 1) * P], ones[:], diag[:, o, :], start=True, stop=True)
                ins.then_inc(tern_psum, 1)

            def products(out, pairs, first=True, last=True):
                for j, (a, b) in enumerate(pairs):
                    ins = mm(out, a, b, start=(first and j == 0), stop=(last and j == len(pairs) - 1))
                return ins

            def transposes(k, b, banks):
                if k < 2:
                    pe.wait_ge(xn_ready[k], upto(b, NT, NT))
                else:
                    pe.wait_ge(sums_ready, upto(b, KC, KC))
                for kc in range(KC):
                    for i in range(NT):
                        ins = nc.tensor.transpose(bank[banks[kc]][:, i * P:(i + 1) * P],
                                                  xn[k][:, i, kc * P:(kc + 1) * P] if k < 2 else sums[:, i, kc, :],
                                                  idf[:])
                    ins.then_inc(xT_psum[k], 1)

            def query(n):
                for mc in range(KC):
                    cols = slice(mc * P, (mc + 1) * P)
                    pairs = []
                    for kc in range(KC):
                        pairs += [(m_hi[:, kc, cols], xT_hi[0][:, kc, :]), (m_hi[:, kc, cols], xT_lo[0][:, kc, :]),
                                  (m_lo[:, kc, cols], xT_hi[0][:, kc, :])]
                    products(bank[2 + mc][:], pairs).then_inc(q_psum, 1)

            def value(n):
                for i in range(NT):
                    rows = slice(i * P, (i + 1) * P)
                    pairs = [(one_rows[:], bias_rows[:])]
                    for kc in range(KC):
                        pairs += [(xT_hi[0][:, kc, rows], wv_hi[:, kc, :]), (xT_hi[0][:, kc, rows], wv_lo[:, kc, :]),
                                  (xT_lo[0][:, kc, rows], wv_hi[:, kc, :])]
                    ins = products(bank[4 + i // 2][:, (i % 2) * C:(i % 2 + 1) * C], pairs)
                    if i % 2:
                        ins.then_inc(v_psum, 1)

            def scores(n, i):
                w = (i + 1) * P
                rows = slice(i * P, w)
                out = bank[2 + i]
                pairs = []
                for kc in range(KC):
                    pairs += [(q_hi[:, kc, rows], xT_hi[0][:, kc, 0:w]), (q_hi[:, kc, rows], xT_lo[0][:, kc, 0:w]),
                              (q_lo[:, kc, rows], xT_hi[0][:, kc, 0:w])]
                products(out[:, 0:w], pairs, last=False)
                mm(out[:, rows], idh[:], msk[:], start=False, stop=True).then_inc(scores_psum, 1)

            def prob_transposes(n, i):
                pe.wait_ge(prob_ready, upto(n, NT, i + 1))
                for j in range(i + 1):
                    ins = nc.tensor.transpose(bank[2 + i][:, j * P:(j + 1) * P], prob[:, i, j * P:(j + 1) * P],
                                              idf[:])
                ins.then_inc(pT_psum, 1)

            def attend(n, i):
                pe.wait_ge(pT_ready, upto(n, NT, i + 1))
                pairs = []
                for j in range(i + 1):
                    cols = slice(j * P, (j + 1) * P)
                    pairs += [(pT_hi[:, i, cols], v_hi[:, j, :]), (pT_hi[:, i, cols], v_lo[:, j, :]),
                              (pT_lo[:, i, cols], v_hi[:, j, :])]
                products(bank[2 + i][:, 0:C], pairs).then_inc(att_psum, 1)

            def hadamard(b, banks=(0, 1)):
                for i in range(NT):
                    rows = slice(i * P, (i + 1) * P)
                    for kc in range(KC):
                        ins = products(bank[banks[i // 2]][:, (i % 2) * C + kc * P:(i % 2) * C + (kc + 1) * P],
                                       [(xT_hi[2][:, kc, rows], had[:]), (xT_lo[2][:, kc, rows], had[:])])
                    if i % 2:
                        ins.then_inc(had_psum, 1)

            def gated_context(b, banks):
                for i in range(NT):
                    rows = slice(i * P, (i + 1) * P)
                    ins = products(bank[banks[i // 2]][:, (i % 2) * C:(i % 2 + 1) * C],
                                   [(ghl[:, rows], ctx_hi[:, b, :]), (ghl[:, rows], ctx_lo[:, b, :])])
                    if i % 2:
                        ins.then_inc(o2_psum, 1)

            def quant_transposes(b):
                for kc in range(KC):
                    for i in range(NT):
                        ins = nc.tensor.transpose(bank[0].bitcast(F16)[:, kc * T + i * P:kc * T + (i + 1) * P],
                                                  quant[:, i, kc * P:(kc + 1) * P], idh[:])
                ins.then_inc(qT_psum, 1)

            def ternary(b, banks):
                for i in range(NT):
                    rows = slice(i * P, (i + 1) * P)
                    ins = products(bank[banks[i // 2]][:, (i % 2) * C:(i % 2 + 1) * C],
                                   [(qT[:, kc, rows], ternT[:, kc, :]) for kc in range(KC)])
                    if i % 2:
                        ins.then_inc(y_psum, 1)

            def context_scores(b):
                pairs = []
                for kc in range(KC):
                    c_hi, c_lo = (t[:, b, kc, :, :].rearrange("p t f -> p (t f)") for t in (cT_hi, cT_lo))
                    pairs += [(c_hi, xT_hi[1][:, kc, :]), (c_hi, xT_lo[1][:, kc, :]), (c_lo, xT_hi[1][:, kc, :])]
                products(bank[6][:], pairs).then_inc(h_psum, 1)

            transposes(0, 0, (0, 1))
            pe.wait_ge(ld_pair, 16)
            context_transposes((0,))
            pe.wait_ge(ld_f16, 48)
            pe.wait_ge(bias_ready, 1)
            pe.wait_ge(w_ready, 1)

            def last_steps(n, stages):
                if stages == "BCD":
                    pe.wait_ge(xT_ready[2], upto(n - 3, KC, KC))
                    hadamard(n - 3)
                    pe.wait_ge(x2_ready, upto(n - 1, NT, NT))
                    pe.wait_ge(g_lo_ready, upto(n - 2, 1, 1))
                    gated_context(n - 2, (2, 3))
                    pe.wait_ge(ytmp_ready, upto(n - 4, NT, NT))
                    transposes(1, n - 1, (6, 7))
                    pe.wait_ge(quant_ready, upto(n - 3, 1, 1))
                    quant_transposes(n - 3)
                    pe.wait_ge(xT_ready[1], upto(n - 1, KC, KC))
                    context_scores(n - 1)
                    pe.wait_ge(qT_ready, upto(n - 3, 1, 1))
                    ternary(n - 3, (4, 5))
                    transposes(2, n - 2, (0, 1))
                    pe.wait_ge(g_lo_ready, upto(n - 1, 1, 1))
                    pe.wait_ge(x3_ready, upto(n - 2, 2, 2))
                    gated_context(n - 1, (2, 3))
                elif stages == "CD":
                    pe.wait_ge(xT_ready[2], upto(n - 3, KC, KC))
                    hadamard(n - 3)
                    pe.wait_ge(quant_ready, upto(n - 3, 1, 1))
                    quant_transposes(n - 3)
                    transposes(2, n - 2, (6, 7))
                    pe.wait_ge(xT_ready[2], upto(n - 2, KC, KC))
                    hadamard(n - 2, (2, 3))
                    pe.wait_ge(ytmp_ready, upto(n - 4, NT, NT))
                    pe.wait_ge(qT_ready, upto(n - 3, 1, 1))
                    ternary(n - 3, (4, 5))
                else:
                    pe.wait_ge(quant_ready, upto(n - 3, 1, 1) + 1)
                    quant_transposes(n - 3)
                    pe.wait_ge(qT_ready, upto(n - 3, 1, 1))
                    ternary(n - 3, (6, 7))

            def body(n, parity, stages):
                if "A" not in stages:
                    last_steps(n, stages)
                    return
                if "A" in stages:
                    if "B" in stages:
                        pe.wait_ge(x2_ready, upto(n - 1, NT, 2))
                    pe.wait_ge(xT_ready[0], upto(n, KC, KC))
                    query(n)
                    if "P" in stages:
                        pe.wait_ge(bias_ready, 2)
                        context_transposes((1,))
                if "D" in stages:
                    pe.wait_ge(xT_ready[2], upto(n - 3, KC, KC))
                    hadamard(n - 3)
                if "A" in stages:
                    if "B" in stages:
                        pe.wait_ge(x2_ready, upto(n - 1, NT, NT))
                    value(n)
                if "C" in stages:
                    pe.wait_ge(g_lo_ready, upto(n - 2, 1, 1))
                    if not (isinstance(n, int) and n < 4):
                        pe.wait_ge(ytmp_ready, upto(n - 4, NT, NT))
                    if "Z" in stages and isinstance(n, int) and n < 4:
                        pe.wait_ge(ctx_ready, B // CQ if "D" in stages else 2)
                    gated_context(n - 2, (6, 7))
                if "A" in stages:
                    pe.wait_ge(q_ready, upto(n, KC, KC))
                    scores(n, 0)
                    scores(n, 1)
                    pe.wait_ge(v_ready, upto(n, 2, 1))
                    scores(n, 2)
                if "D" in stages:
                    pe.wait_ge(quant_ready, upto(n - 3, 1, 1))
                    quant_transposes(n - 3)
                if "A" in stages:
                    pe.wait_ge(v_ready, upto(n, 2, 2))
                    scores(n, 3)
                    if "P" in stages:
                        context_transposes((2, 3))
                    prob_transposes(n, 0)
                if "B" in stages:
                    if "C" in stages:
                        pe.wait_ge(x3_ready, upto(n - 2, 2, 2))
                    transposes(1, n - 1, (6, 7))
                if "Z" in stages:
                    if "Q" in stages:
                        pe.wait_ge(tern_taken, 2)
                    if "D" in stages:
                        pe.wait_ge(qT_ready, upto(n - 3, 1, 1))
                    transposes(0, n + 1, (0, 1))
                if "A" in stages:
                    attend(n, 0)
                    prob_transposes(n, 1)
                if "D" in stages:
                    pe.wait_ge(qT_ready, upto(n - 3, 1, 1))
                    pe.wait_ge(xT_ready[1], upto(n - 1, KC, KC))
                    ternary(n - 3, (6, 7))
                if "A" in stages:
                    prob_transposes(n, 2)
                    prob_transposes(n, 3)
                if "B" in stages:
                    pe.wait_ge(xT_ready[1], upto(n - 1, KC, KC))
                    if "Q" in stages:
                        pe.wait_ge(cT_ready, 2)
                    if "D" in stages:
                        pe.wait_ge(ytmp_ready, upto(n - 3, NT, 2))
                    context_scores(n - 1)
                if "A" in stages:
                    attend(n, 1)
                    attend(n, 2)
                    attend(n, 3)
                if "C" in stages:
                    if "Z" in stages:
                        pe.wait_ge(xT_ready[0], upto(n + 1, KC, KC))
                    transposes(2, n - 2, (0, 1))
                if "P" in stages:
                    pe.wait_ge(xT_ready[0], upto(1, KC, KC))
                    ternary_transposes()
            steps(pe, body)


def kernel(x, ctx_1024, L0_attn_Wq, L0_attn_bq, L0_attn_Wk, L0_attn_bk, L0_attn_Wv, L0_attn_bv, L0_ffn_weight):
    import concourse.bacc as bacc
    from concourse.bass_utils import run_bass_kernel_spmd

    C = x.shape[-1]
    signs = np.array([[1.0]])
    while signs.shape[0] < C // 2:
        signs = np.block([[signs, signs], [signs, -signs]])
    later = np.triu(np.ones((P, P)), 1) * MASKED
    consts = {
        "hada": signs.astype(np.float16),
        "ident": np.eye(P, dtype=np.float32),
        "ident16": np.eye(P, dtype=np.float16),
        "mask": later.astype(mybir.dt.np(BF16)),
    }
    data = {
        "x": x, "ctx_kv": ctx_1024, "wq": L0_attn_Wq, "bq": np.reshape(L0_attn_bq, (-1, P)).T, "wk": L0_attn_Wk, "wv": L0_attn_Wv,
        "bv": L0_attn_bv, "wffn": L0_ffn_weight,
    }
    nc = bacc.Bacc("TRN2", target_bir_lowering=False, num_devices=1)
    arrays, aps = {}, {}
    for name, a in {**data, **consts}.items():
        a = np.ascontiguousarray(a)
        arrays[f"in_{name}"] = a
        aps[name] = nc.dram_tensor(f"in_{name}", a.shape, mybir.dt.from_np(a.dtype), kind="ExternalInput").ap()
    aps["y"] = nc.dram_tensor("out_y", x.shape, F32, kind="ExternalOutput").ap()
    build(nc, **aps)
    r = run_bass_kernel_spmd(nc, [arrays], core_ids=[0])
    return r.results[0]["out_y"]
```
